# Optimizing a Trainium2 kernel written in Bass

```python
import numpy as np
import jax
import jax.numpy as jnp

def _softmax(x, axis=-1):
    return jax.nn.softmax(x, axis=axis)

def _gelu(x):
    return jax.nn.gelu(x, approximate=True)

def _silu(x):
    return jax.nn.silu(x)

def _sigmoid(x):
    return jax.nn.sigmoid(x)

def _layernorm(x, axis=-1, eps=1e-05):
    m = jnp.mean(x, axis=axis, keepdims=True)
    v = jnp.var(x, axis=axis, keepdims=True)
    return (x - m) / jnp.sqrt(v + eps)

def _scatter_add(tgt, idx, src, axis=0):
    return tgt.at[idx].add(src)

def _segment_sum(src, seg, n):
    return jax.ops.segment_sum(src, seg, n)
kernel_name = 'mk_xattn_ffn_d1_seqx_r2_e8bc42'

def setup_inputs(seed: int=0):
    np.random.seed(seed)
    _w = jnp.asarray

    def _rec_inputs():
        import jax
        import jax.numpy as jnp
        _rk = jax.random.key(seed)
        x = -0.0003929 + 0.9999 * jax.random.normal(jax.random.fold_in(_rk, 1), (4, 1024, 512), jnp.float32)
        _lenS = 1024 - jax.random.randint(jax.random.fold_in(_rk, 7), (4,), 0, max(1, 1024 // 4) + 1, jnp.int32)
        _lenS2 = 1024 - jax.random.randint(jax.random.fold_in(_rk, 8), (4,), 0, max(1, 1024 // 4) + 1, jnp.int32)
        _ctx_1024P = jax.random.normal(jax.random.fold_in(_rk, 11), (4, 16, 512), jnp.float32)
        _ctx_1024c = jax.random.dirichlet(jax.random.fold_in(_rk, 511), 0.3 * jnp.ones((16,), jnp.float32), (4, 1024))
        _ctx_1024t = jnp.einsum('bsk,bkd->bsd', _ctx_1024c, _ctx_1024P)
        _ctx_1024t = _ctx_1024t * jax.lax.rsqrt(jnp.mean(jnp.square(_ctx_1024t)) + 1e-12) * 0.953939
        ctx_1024 = 2.81802e-05 + 1.00001 * (_ctx_1024t + 0.3 * jax.random.normal(jax.random.fold_in(_rk, 611), (4, 1024, 512), jnp.float32))
        _validS = jnp.arange(1024)[None, :] < _lenS[:, None]
        _validS2 = jnp.arange(1024)[None, :] < _lenS2[:, None]
        _causal = jnp.tril(jnp.ones((1024, 1024), dtype=bool))
        mask_BxS2_bf1 = jnp.ones((4, 1024), dtype=bool)
        return (x, ctx_1024, mask_BxS2_bf1)
    x, ctx_1024, mask_BxS2_bf1 = _rec_inputs()

    def _L0_xattn_setup():
        import jax, jax.numpy as jnp
        import numpy as np
        WINDOW_SIZE = 128
        NEG_INF = -1000000000.0
        key = jax.random.key(seed)
        kq, kk, kv = jax.random.split(key, 3)
        B, S, E = (4, 2048, 512)
        query = jax.random.normal(kq, (B, S, E), dtype=jnp.float32)
        k_ = jax.random.normal(kk, (B, S, E), dtype=jnp.float32)
        value = jax.random.normal(kv, (B, S, E), dtype=jnp.float32)
        mask = jnp.ones((B, S), dtype=bool)
        return {'query': query, 'key': k_, 'value': value, 'mask': mask}
    _L0_xattn_all = _L0_xattn_setup()
    _L0_xattn_in = {k: v for k, v in _L0_xattn_all.items() if k in ()}
    del _L0_xattn_all

    def _L0_ffn_setup():
        import jax, jax.numpy as jnp
        import numpy as np
        DIM = 512
        DEPTH = 2
        HEADS = 8
        DIM_HEAD = 64
        WINDOW = 256
        INNER = HEADS * DIM_HEAD
        HID = int(DIM * 4 * 2 / 3)
        B, N = (2, 4096)
        QK_SCALE = 8.0

        def shift_token(t):
            t1, t2 = jnp.split(t, 2, axis=-1)
            t2 = jnp.pad(t2, ((0, 0), (1, 0), (0, 0)))[:, :-1]
            return jnp.concatenate([t1, t2], axis=-1)

        def l2norm(t):
            return t / jnp.clip(jnp.linalg.norm(t, axis=-1, keepdims=True), 1e-12)

        def rotate_half(x):
            x1, x2 = jnp.split(x, 2, axis=-1)
            return jnp.concatenate([-x2, x1], axis=-1)

        def rotary_xpos(q, k):
            n = q.shape[-2]
            half_idx = jnp.arange(0, DIM_HEAD, 2, dtype=jnp.float32)
            inv_freq = 1.0 / 10000.0 ** (half_idx / DIM_HEAD)
            t = jnp.arange(n, dtype=jnp.float32)
            freqs = t[:, None] * inv_freq[None, :]
            freqs = jnp.concatenate([freqs, freqs], axis=-1)
            base = (half_idx + 0.4 * DIM_HEAD) / (1.4 * DIM_HEAD)
            power = (t - n // 2) / float(WINDOW // 2)
            scale = base[None, :] ** power[:, None]
            scale = jnp.concatenate([scale, scale], axis=-1)
            cos, sin = (jnp.cos(freqs), jnp.sin(freqs))
            q = q * cos * scale + rotate_half(q) * sin * scale
            k = k * cos / scale + rotate_half(k) * sin / scale
            return (q, k)

        def local_attention(q, k, v):
            b, h, n, d = q.shape
            w = n // WINDOW
            bq = q.reshape(b, h, w, WINDOW, d) * QK_SCALE
            bk = k.reshape(b, h, w, WINDOW, d)
            bv = v.reshape(b, h, w, WINDOW, d)

            def look_around(t):
                p = jnp.pad(t, ((0, 0), (0, 0), (1, 0), (0, 0), (0, 0)))
                return jnp.concatenate([p[:, :, :w], p[:, :, 1:]], axis=3)
            bk, bv = (look_around(bk), look_around(bv))
            bt = jnp.arange(n).reshape(w, WINDOW)
            btp = jnp.pad(bt, ((1, 0), (0, 0)), constant_values=-1)
            btk = jnp.concatenate([btp[:w], btp[1:]], axis=1)
            sim = jnp.einsum('bhwid,bhwjd->bhwij', bq, bk)
            i = bt[:, :, None]
            j = btk[:, None, :]
            mask = (i < j) | (i > j + WINDOW) | (j == -1)
            sim = jnp.where(mask, -jnp.finfo(sim.dtype).max, sim)
            attn = jax.nn.softmax(sim, axis=-1)
            out = jnp.einsum('bhwij,bhwjd->bhwid', attn, bv)
            return out.reshape(b, h, n, d)

        def _layer(x, wqkv, qs, ksc, wo, lg, lb, w1, b1, w2, b2):
            b, n, _ = x.shape
            h = shift_token(x)
            qkv = h @ wqkv
            q, k, v = jnp.split(qkv, 3, axis=-1)
            to_heads = lambda t: t.reshape(b, n, HEADS, DIM_HEAD).transpose(0, 2, 1, 3)
            q, k, v = (to_heads(q), to_heads(k), to_heads(v))
            q = l2norm(q) * qs
            k = l2norm(k) * ksc
            q, k = rotary_xpos(q, k)
            o = local_attention(q, k, v)
            o = o.transpose(0, 2, 1, 3).reshape(b, n, INNER)
            x = x + o @ wo
            h = shift_token(x)
            mu = h.mean(-1, keepdims=True)
            var = h.var(-1, keepdims=True)
            h = (h - mu) / jnp.sqrt(var + 1e-05) * lg + lb
            h = h @ w1 + b1
            a, g = jnp.split(h, 2, axis=-1)
            h = a * jax.nn.gelu(g, approximate=False)
            x = x + h @ w2 + b2
            return x
        key = jax.random.key(seed)
        ks = jax.random.split(key, 6)
        return {'x': jax.random.normal(ks[0], (B, N, DIM), jnp.float32), 'wqkv': jax.random.normal(ks[1], (DEPTH, DIM, 3 * INNER), jnp.float32) * 0.02, 'q_scale': jnp.ones((DEPTH, DIM_HEAD), jnp.float32), 'k_scale': jnp.ones((DEPTH, DIM_HEAD), jnp.float32), 'wo': jax.random.normal(ks[2], (DEPTH, INNER, DIM), jnp.float32) * 0.02, 'ln_g': jnp.ones((DEPTH, DIM), jnp.float32), 'ln_b': jnp.zeros((DEPTH, DIM), jnp.float32), 'w1': jax.random.normal(ks[3], (DEPTH, DIM, 2 * HID), jnp.float32) * 0.02, 'b1': jnp.zeros((DEPTH, 2 * HID), jnp.float32), 'w2': jax.random.normal(ks[4], (DEPTH, HID, DIM), jnp.float32) * 0.02, 'b2': jnp.zeros((DEPTH, DIM), jnp.float32)}
    _L0_ffn_all = _L0_ffn_setup()
    _L0_ffn_in = {k: v for k, v in _L0_ffn_all.items() if k in ('wqkv', 'q_scale', 'k_scale', 'wo', 'ln_g', 'ln_b', 'w1', 'b1', 'w2', 'b2')}
    del _L0_ffn_all
    return {'x': x, 'ctx_1024': ctx_1024, 'mask_BxS2_bf1': mask_BxS2_bf1, 'L0_ffn_wqkv': _L0_ffn_in['wqkv'], 'L0_ffn_q_scale': _L0_ffn_in['q_scale'], 'L0_ffn_k_scale': _L0_ffn_in['k_scale'], 'L0_ffn_wo': _L0_ffn_in['wo'], 'L0_ffn_ln_g': _L0_ffn_in['ln_g'], 'L0_ffn_ln_b': _L0_ffn_in['ln_b'], 'L0_ffn_w1': _L0_ffn_in['w1'], 'L0_ffn_b1': _L0_ffn_in['b1'], 'L0_ffn_w2': _L0_ffn_in['w2'], 'L0_ffn_b2': _L0_ffn_in['b2']}

def reference(x, ctx_1024, mask_BxS2_bf1, L0_ffn_wqkv, L0_ffn_q_scale, L0_ffn_k_scale, L0_ffn_wo, L0_ffn_ln_g, L0_ffn_ln_b, L0_ffn_w1, L0_ffn_b1, L0_ffn_w2, L0_ffn_b2):
    import jax
    import jax.numpy as jnp

    def _L0_xattn_ref(query, key, value, mask):
        import jax, jax.numpy as jnp
        import numpy as np
        WINDOW_SIZE = 128
        NEG_INF = -1000000000.0
        B, S, E = query.shape
        scale = 1.0 / jnp.sqrt(jnp.asarray(E, dtype=query.dtype))
        scores = jnp.einsum('bqe,bke->bqk', query, key) * scale
        idx = jnp.arange(S)
        band = jnp.abs(idx[:, None] - idx[None, :]) <= WINDOW_SIZE
        allowed = band[None, :, :] & mask[:, None, :]
        scores = jnp.where(allowed, scores, NEG_INF)
        probs = jax.nn.softmax(scores, axis=-1)
        out = jnp.einsum('bqk,bke->bqe', probs, value)
        return out

    def _L0_ffn_ref(x, wqkv, q_scale, k_scale, wo, ln_g, ln_b, w1, b1, w2, b2):
        import jax, jax.numpy as jnp
        import numpy as np
        DIM = 512
        DEPTH = 2
        HEADS = 8
        DIM_HEAD = 64
        WINDOW = 256
        INNER = HEADS * DIM_HEAD
        HID = int(DIM * 4 * 2 / 3)
        B, N = (2, 4096)
        QK_SCALE = 8.0

        def shift_token(t):
            t1, t2 = jnp.split(t, 2, axis=-1)
            t2 = jnp.pad(t2, ((0, 0), (1, 0), (0, 0)))[:, :-1]
            return jnp.concatenate([t1, t2], axis=-1)

        def l2norm(t):
            return t / jnp.clip(jnp.linalg.norm(t, axis=-1, keepdims=True), 1e-12)

        def rotate_half(x):
            x1, x2 = jnp.split(x, 2, axis=-1)
            return jnp.concatenate([-x2, x1], axis=-1)

        def rotary_xpos(q, k):
            n = q.shape[-2]
            half_idx = jnp.arange(0, DIM_HEAD, 2, dtype=jnp.float32)
            inv_freq = 1.0 / 10000.0 ** (half_idx / DIM_HEAD)
            t = jnp.arange(n, dtype=jnp.float32)
            freqs = t[:, None] * inv_freq[None, :]
            freqs = jnp.concatenate([freqs, freqs], axis=-1)
            base = (half_idx + 0.4 * DIM_HEAD) / (1.4 * DIM_HEAD)
            power = (t - n // 2) / float(WINDOW // 2)
            scale = base[None, :] ** power[:, None]
            scale = jnp.concatenate([scale, scale], axis=-1)
            cos, sin = (jnp.cos(freqs), jnp.sin(freqs))
            q = q * cos * scale + rotate_half(q) * sin * scale
            k = k * cos / scale + rotate_half(k) * sin / scale
            return (q, k)

        def local_attention(q, k, v):
            b, h, n, d = q.shape
            w = n // WINDOW
            bq = q.reshape(b, h, w, WINDOW, d) * QK_SCALE
            bk = k.reshape(b, h, w, WINDOW, d)
            bv = v.reshape(b, h, w, WINDOW, d)

            def look_around(t):
                p = jnp.pad(t, ((0, 0), (0, 0), (1, 0), (0, 0), (0, 0)))
                return jnp.concatenate([p[:, :, :w], p[:, :, 1:]], axis=3)
            bk, bv = (look_around(bk), look_around(bv))
            bt = jnp.arange(n).reshape(w, WINDOW)
            btp = jnp.pad(bt, ((1, 0), (0, 0)), constant_values=-1)
            btk = jnp.concatenate([btp[:w], btp[1:]], axis=1)
            sim = jnp.einsum('bhwid,bhwjd->bhwij', bq, bk)
            i = bt[:, :, None]
            j = btk[:, None, :]
            mask = (i < j) | (i > j + WINDOW) | (j == -1)
            sim = jnp.where(mask, -jnp.finfo(sim.dtype).max, sim)
            attn = jax.nn.softmax(sim, axis=-1)
            out = jnp.einsum('bhwij,bhwjd->bhwid', attn, bv)
            return out.reshape(b, h, n, d)

        def _layer(x, wqkv, qs, ksc, wo, lg, lb, w1, b1, w2, b2):
            b, n, _ = x.shape
            h = shift_token(x)
            qkv = h @ wqkv
            q, k, v = jnp.split(qkv, 3, axis=-1)
            to_heads = lambda t: t.reshape(b, n, HEADS, DIM_HEAD).transpose(0, 2, 1, 3)
            q, k, v = (to_heads(q), to_heads(k), to_heads(v))
            q = l2norm(q) * qs
            k = l2norm(k) * ksc
            q, k = rotary_xpos(q, k)
            o = local_attention(q, k, v)
            o = o.transpose(0, 2, 1, 3).reshape(b, n, INNER)
            x = x + o @ wo
            h = shift_token(x)
            mu = h.mean(-1, keepdims=True)
            var = h.var(-1, keepdims=True)
            h = (h - mu) / jnp.sqrt(var + 1e-05) * lg + lb
            h = h @ w1 + b1
            a, g = jnp.split(h, 2, axis=-1)
            h = a * jax.nn.gelu(g, approximate=False)
            x = x + h @ w2 + b2
            return x
        for l in range(DEPTH):
            x = _layer(x, wqkv[l], q_scale[l], k_scale[l], wo[l], ln_g[l], ln_b[l], w1[l], b1[l], w2[l], b2[l])
        return x
    x = x + _L0_xattn_ref(_layernorm(x, axis=-1), ctx_1024, ctx_1024, mask_BxS2_bf1)
    x = x + _L0_ffn_ref(_layernorm(x, axis=-1), L0_ffn_wqkv, L0_ffn_q_scale, L0_ffn_k_scale, L0_ffn_wo, L0_ffn_ln_g, L0_ffn_ln_b, L0_ffn_w1, L0_ffn_b1, L0_ffn_w2, L0_ffn_b2)
    return x

_drawn_inputs = setup_inputs


def setup_inputs(seed=0):
    import zlib

    import numpy as np

    out = dict(_drawn_inputs(seed))
    spreads = {'L0_ffn_q_scale': (1.0, 0.6),
     'L0_ffn_k_scale': (1.0, 0.6),
     'L0_ffn_ln_g': (1.0, 0.6),
     'L0_ffn_ln_b': (0.0, 0.8),
     'L0_ffn_b1': (0.0, 0.413),
     'L0_ffn_b2': (0.0, 0.1)}
    factors = {}
    for name, (base, spread) in spreads.items():
        noise = np.random.default_rng([zlib.crc32(name.encode()), seed]).standard_normal(out[name].shape)
        drawn = base * np.exp(spread * noise) if base else spread * noise
        out[name] = jnp.asarray(drawn.astype(out[name].dtype))
    for name, factor in factors.items():
        out[name] = (out[name] * factor).astype(out[name].dtype)
    return out
```

```python
import numpy as np
import concourse.bass as bass
from concourse import mybir
from concourse.alu_op_type import AluOpType as ALU

F32 = mybir.dt.float32
F32R = mybir.dt.float32r
U8 = mybir.dt.uint8
ACT = mybir.ActivationFunctionType
AX = mybir.AxisListType.X

P = 128
BATCH, SEQ, DIM = 4, 1024, 512
TPB = SEQ // P
TILES = BATCH * TPB
HALF = DIM // 2
KC = DIM // P
HEADS, HD = 8, 64
QKV = 3 * HEADS * HD
HID = int(DIM * 4 * 2 / 3)
DEPTH = 2
HC = (HID + P - 1) // P
GROUP = 4
GROUPS = TILES // GROUP
QK_SCALE = 8.0
EPS = 1e-5
NORM_FLOOR = 1e-12
MASKED = -1e9
BIG = 3.0e38
BAND_SCALE = float(np.float32(1.0) / np.sqrt(np.float32(DIM)))
WIN = 3 * P
FREE_BASE = 16512


def hid_rows(j):
    return min(P, HID - j * P)


class Signal:

    def __init__(self, sem):
        self.sem, self.value = sem, 0


class Queue:

    def __init__(self, signals):
        self.steps, self.passed, self.signals = [], {}, signals

    def wait(self, *marks):
        for mark in marks:
            if mark is None:
                continue
            if isinstance(mark, list):
                self.wait(*mark)
                continue
            signal, value = mark
            if self.passed.get(signal, 0) < value:
                self.passed[signal] = value
                self.steps.append(("wait", signal.sem, value))

    def do(self, build, signal=None, by=1):
        if signal is None:
            self.steps.append(("do", build, None, 0))
            return None
        s = self.signals(signal)
        s.value += by
        self.steps.append(("do", build, s.sem, by))
        return (s, s.value)

    def run(self, engine):
        for kind, what, *rest in self.steps:
            if kind == "wait":
                engine.wait_ge(what, rest[0])
            else:
                ins = what(engine)
                if rest[0] is not None:
                    ins.then_inc(rest[0], rest[1])


class Slot:

    def __init__(self, ap):
        self.ap, self.free = ap, []


class Ring:
    def __init__(self, slots):
        self.slots, self.n = slots, 0

    def next(self):
        self.n += 1
        return self.slots[(self.n - 1) % len(self.slots)]


def build(nc, x, ctx, mask, wqkv, q_scale, k_scale, wo, ln_g, ln_b, w1, b1, w2, b2, consts, out):
    signals = {}

    def signal(name):
        if name not in signals:
            signals[name] = Signal(nc.alloc_semaphore(name))
        return signals[name]

    sp, pe, act, dve, pool = (Queue(signal) for _ in range(5))

    class Plan:

        def __init__(self, start):
            self.at = start

        def tensor(self, name, shape, dtype=F32):
            size = int(np.prod(shape[1:])) * (1 if dtype == U8 else 4)
            t = nc.alloc_sbuf_tensor_at(name, shape, dtype, offset=self.at)
            self.at += (size + 31) // 32 * 32
            return t

        def pair(self, name, shape):
            at = self.at
            t = self.tensor(name, shape, F32R)
            raw = nc.alloc_sbuf_tensor_at(name + "_raw", shape, F32, offset=at)
            return t, raw

    fixed = Plan(FREE_BASE)
    ident = fixed.tensor("ident", [P, P])
    half_power = fixed.tensor("half_power", [P, 16])
    masked_col = fixed.tensor("masked_col", [P, 1])
    stats = fixed.tensor("stats", [P, 2, 32])
    small = fixed.tensor("small", [P, 4, 32])
    norm = fixed.tensor("norm", [P, 2, 32])
    phase_base = fixed.at

    bank_pair = nc.alloc_psum_tensor("bank_pair", [P, 2, 512], F32)[:, :, :]
    banks = [nc.alloc_psum_tensor(f"bank{i}", [P, 512], F32)[:, :] for i in range(6)]

    x1_dram = nc.dram_tensor("x1_dram", [BATCH, SEQ, DIM], F32).ap()
    stream = [nc.dram_tensor(f"stream{i}", [BATCH, SEQ + 1, DIM], F32).ap() for i in range(2 * DEPTH)]
    zero_rows = [sp.do(lambda e, s=s: e.dma_start(s[:, 0, :], consts["zeros"]), "zero_rows", 16)
                 for s in stream]
    x1_stored = [None] * TILES
    stream_stored = [[None] * TILES for _ in stream]

    def rows(t):
        return t // TPB, (t % TPB) * P

    m_ident = sp.do(lambda e: e.dma_start(ident[:, :], consts["ident"]), "ident_in", 16)
    m_half = pool.do(lambda e: e.memset(half_power[:, :], -0.5), "half_power")
    m_masked = pool.do(lambda e: e.memset(masked_col[:, :], MASKED), "masked_col")
    pool.wait(m_half)
    act.wait(m_masked)
    pe.wait(m_ident)

    def split_weight(queue_sub, h, l, raw, loaded, name):
        act.wait(loaded)
        rounded = act.do(lambda e: e.activation(l, raw, ACT.Copy), name + "_round")
        dve.wait(rounded)
        low = dve.do(lambda e: e.tensor_tensor(l, raw, l.bitcast(F32), ALU.subtract), name + "_low")
        act.wait(low)
        return act.do(lambda e: e.activation(h, raw, ACT.Copy), name + "_high")

    def transposes(bank, sources, name):
        pe.wait(bank.free)
        for i, src in enumerate(sources):
            r = lambda e, i=i, src=src: e.transpose(bank.ap[:, i * P:(i + 1) * P], src, ident[:, :])
            mark = pe.do(r, name if i == len(sources) - 1 else None)
        return mark

    def split_bank(bank, turned, high, low, free, name):
        act.wait(turned, free)
        m_high = act.do(lambda e: e.activation(high, bank.ap, ACT.Copy), name + "_high")
        dve.wait(m_high, turned, free)
        m_low = dve.do(lambda e: e.tensor_tensor(low, bank.ap, high.bitcast(F32), ALU.subtract), name + "_low")
        bank.free = [m_low]
        return [m_high, m_low]

    def products(bank, lhs, rhs, n, first=True, last=True):
        out_ap = bank
        return [lambda e, a=a, b=b, s=s, p=p: e.matmul(out_ap, a, b, start=s, stop=p)
                for a, b, s, p in ((lhs[0], rhs[0], first, False), (lhs[1], rhs[0], False, False),
                                   (lhs[0], rhs[1], False, last))]

    def layer_norm(src, pieces, dst, ready, k, name):
        st = stats[:, k, :]
        dve.wait(ready)
        for i, piece in enumerate(pieces):
            m = dve.do(lambda e, i=i, piece=piece: e.bn_stats(st[:, 6 * i:6 * i + 6], piece), name + "_stats")
        dve.wait(m)
        m = dve.do(lambda e: e.bn_aggr(st[:, 12:14], st[:, 0:6 * len(pieces)]), name + "_moments")
        pool.wait(m)
        m = pool.do(lambda e: e.tensor_scalar(st[:, 14:15], st[:, 13:14], 1.0, EPS, ALU.mult, ALU.add), name + "_var")
        pool.wait(m)
        m = pool.do(lambda e: e.tensor_tensor(st[:, 15:16], st[:, 14:15], half_power[:, 0:1], ALU.pow), name + "_rstd")
        dve.wait(m)
        return dve.do(lambda e: e.tensor_scalar(dst, src, st[:, 12:13], st[:, 15:16], ALU.subtract, ALU.mult),
                      name + "_normed")

    attend_plan = Plan(phase_base)
    wqkv_h, wqkv_raw = attend_plan.pair("wqkv_h", [P, KC, QKV])
    wqkv_l = attend_plan.tensor("wqkv_l", [P, KC, QKV], F32R)
    wo_h, wo_raw = attend_plan.pair("wo_h", [P, KC, DIM])
    wo_l = attend_plan.tensor("wo_l", [P, KC, DIM], F32R)
    attend_weights_end = attend_plan.at

    def load_attend_weights(l, free):
        ready = []
        sp.wait(free)
        act.wait(free)
        wq = wqkv[l].rearrange("(c p) n -> p c n", p=P)
        for part in (2, 0, 1):
            cols = slice(part * DIM, (part + 1) * DIM)
            loaded = sp.do(lambda e, cols=cols: e.dma_start(wqkv_raw[:, :, cols], wq[:, :, cols]), f"wqkv_in{part}", 16)
            ready.append(split_weight(dve, wqkv_h[:, :, cols], wqkv_l[:, :, cols], wqkv_raw[:, :, cols], loaded, "weight"))
        loaded = sp.do(lambda e: e.dma_start(wo_raw[:, :, :], wo[l].rearrange("(c p) n -> p c n", p=P)), "wo_in", 16)
        ready.append(split_weight(dve, wo_h[:, :, :], wo_l[:, :, :], wo_raw[:, :, :], loaded, "weight"))
        return ready

    def band_phase():
        plan = Plan(attend_weights_end)
        ctx_h = plan.tensor("ctx_h", [P, TPB, DIM], F32R)
        ctx_l = plan.tensor("ctx_l", [P, TPB, DIM], F32R)
        keyT_h = plan.tensor("keyT_h", [P, KC, SEQ], F32R)
        keyT_l = plan.tensor("keyT_l", [P, KC, SEQ], F32R)
        ctx_in = Ring([Slot(plan.tensor(f"ctx_in{i}", [P, DIM])) for i in range(3)])
        sum_in = Ring([Slot(plan.tensor(f"sum_in{i}", [P, DIM])) for i in range(2)])
        x_in = Ring([Slot(plan.tensor(f"x_in{i}", [P, DIM])) for i in range(5)])
        xn = plan.tensor("xn", [P, DIM])
        queryT = Ring([Slot(plan.tensor(f"queryT{i}", [P, 2, DIM], F32R)) for i in range(2)])
        ctx_sum = Slot(plan.tensor("ctx_sum", [P, DIM]))
        total = Ring([Slot(plan.tensor(f"ctx_total{i}", [P, DIM])) for i in range(2)])
        ones = plan.tensor("ones", [P, P])
        band01 = plan.tensor("band01", [P, WIN])
        key_mask = plan.tensor("key_mask", [P, SEQ], U8)
        key01 = plan.tensor("key01", [P, SEQ])
        keep = Slot(plan.tensor("keep", [P, WIN]))
        put = Slot(plan.tensor("put", [P, WIN]))
        score = Slot(plan.tensor("score", [P, WIN]))
        prob = Ring([Slot(plan.tensor(f"prob{i}", [P, WIN])) for i in range(2)])
        probT = plan.tensor("probT", [P, 2, WIN], F32R)
        mixed = plan.tensor("mixed", [P, DIM])
        x1_out = Ring([Slot(plan.tensor(f"x1_out{i}", [P, DIM])) for i in range(2)])
        s_out = Ring([Slot(plan.tensor(f"s_out{i}", [P, DIM])) for i in range(2)])
        turn_banks = Ring([Slot(banks[0]), Slot(banks[1])])
        score_bank = Ring([Slot(banks[2]), Slot(banks[3])])
        probT_bank = Slot(banks[4])
        out_bank = Slot(banks[5])
        total_bank = Slot(bank_pair[:, 0, :])

        m_ones = pool.do(lambda e: e.memset(ones[:, :], 1.0), "ones")
        m_band = sp.do(lambda e: e.dma_start(band01[:, :], consts["band01"]), "band01_in", 16)
        st = {"probT_free": None, "xn_free": None, "mixed": None, "key01_free": [], "mask_free": None}
        ctx_ready, read_by = [None] * TILES, [None] * TILES
        x_tile, q_ready, q_slot, totals = {}, {}, {}, {}
        soft = {}

        def load_x(t):
            b, r = rows(t)
            slot = x_in.next()
            sp.wait(slot.free)
            n = t % 5
            x_tile[t] = (slot, sp.do(lambda e: e.dma_start(slot.ap[:, :], x[b, r:r + P, :]), f"x_in{n}", 16))

        def prepare_ctx(t):
            b, r = rows(t)
            slot, k = ctx_in.next(), t % TPB
            sp.wait(slot.free)
            loaded = sp.do(lambda e: e.dma_start(slot.ap[:, :], ctx[b, r:r + P, :]), f"ctx_in{t % 3}", 16)
            pe.wait(loaded)
            bank = turn_banks.next()
            turned = transposes(bank, [slot.ap[:, c * P:(c + 1) * P] for c in range(KC)], "ctx_turned")
            old = [read_by[t - TPB + 1]] if t >= TPB else []
            bank4 = Slot(bank.ap[:, :].rearrange("p (c n) -> p c n", c=KC))
            key_marks = split_bank(bank4, turned, keyT_h[:, :, k * P:(k + 1) * P], keyT_l[:, :, k * P:(k + 1) * P],
                                   old, "keyT")
            bank.free = bank4.free
            act.wait(loaded)
            m_h = act.do(lambda e: e.activation(ctx_h[:, k, :], slot.ap[:, :], ACT.Copy), "ctx_high")
            pool.wait(m_h)
            m_l = pool.do(lambda e: e.tensor_tensor(ctx_l[:, k, :], slot.ap[:, :], ctx_h[:, k, :].bitcast(F32),
                                                    ALU.subtract), "ctx_low")
            slot.free = [turned, m_h, m_l]
            ctx_ready[t] = key_marks + [m_h, m_l]

        def prepare_batch(b):
            for k in range(TPB):
                slot = sum_in.next()
                sp.wait(slot.free)
                n = (sum_in.n - 1) % 2
                loaded = sp.do(lambda e, k=k, slot=slot: e.dma_start(slot.ap[:, :], ctx[b, k * P:(k + 1) * P, :]),
                               f"sum_in{n}", 16)
                pool.wait(loaded)
                if k == 0:
                    pool.wait(ctx_sum.free)
                    m = pool.do(lambda e, slot=slot: e.tensor_copy(ctx_sum.ap[:, :], slot.ap[:, :]), "ctx_sum")
                else:
                    pool.wait(m)
                    m = pool.do(lambda e, slot=slot: e.tensor_tensor(ctx_sum.ap[:, :], ctx_sum.ap[:, :], slot.ap[:, :],
                                                                     ALU.add), "ctx_sum")
                slot.free = [m]
            pe.wait(m, m_ones, total_bank.free)
            m = pe.do(lambda e: e.matmul(total_bank.ap, ones[:, :], ctx_sum.ap[:, :], start=True, stop=True), "total")
            ctx_sum.free = [m]
            slot = total.next()
            act.wait(m, slot.free)
            m = act.do(lambda e: e.activation(slot.ap[:, :], total_bank.ap, ACT.Copy), "total_out")
            total_bank.free = [m]
            totals[b] = (slot, m)

        def load_mask(b):
            sp.wait(st["mask_free"])
            loaded = sp.do(lambda e: e.dma_start(key_mask[:, :], mask[b].partition_broadcast(P)), "mask_in", 16)
            pool.wait(loaded, st["key01_free"])
            st["mask_free"] = st["key01"] = pool.do(lambda e: e.tensor_copy(key01[:, :], key_mask[:, :]), "key01")

        def query(t):
            slot, loaded = x_tile[t]
            dve.wait(st["xn_free"])
            m = layer_norm(slot.ap[:, :], [slot.ap[:, :]], xn[:, :], loaded, 0, "ln")
            pe.wait(m)
            bank = turn_banks.next()
            turned = transposes(bank, [xn[:, c * P:(c + 1) * P] for c in range(KC)], "x_turned")
            st["xn_free"] = turned
            q = queryT.next()
            q_slot[t] = q
            q_ready[t] = split_bank(bank, turned, q.ap[:, 0, :], q.ap[:, 1, :], q.free, "queryT")

        def window(t):
            k = t % TPB
            lo, hi = max(k - 1, 0), min(k + 1, TPB - 1)
            return lo, hi, (hi - lo + 1) * P, (lo - (k - 1)) * P

        def scores(t):
            k = t % TPB
            lo, hi, n, off = window(t)
            base = t - k
            if k == 0:
                load_mask(t // TPB)
            pool.wait(st["key01"], m_band, keep.free)
            m_keep = pool.do(lambda e: e.tensor_tensor(keep.ap[:, 0:n], band01[:, off:off + n],
                                                       key01[:, lo * P:lo * P + n], ALU.mult), "keep")
            st["key01_free"] = [m_keep]
            pool.wait(m_keep, put.free)
            m_put = pool.do(lambda e: e.tensor_scalar(put.ap[:, 0:n], keep.ap[:, 0:n], -MASKED, MASKED,
                                                      ALU.mult, ALU.add), "put")
            bank, q = score_bank.next(), q_slot[t]
            pe.wait(q_ready[t], [ctx_ready[base + i] for i in range(lo, hi + 1)], bank.free)
            keys = slice(lo * P, (hi + 1) * P)
            for c in range(KC):
                for f in products(bank.ap[:, 0:n], [q.ap[:, i, c * P:(c + 1) * P] for i in (0, 1)],
                                  (keyT_h[:, c, keys], keyT_l[:, c, keys]), n, c == 0, c == KC - 1):
                    m = pe.do(f, "scores")
            q.free = [m]
            sm = small[:, t % 2, :]
            dve.wait(m, m_keep, score.free)
            m = dve.do(lambda e: e.scalar_tensor_tensor(out=score.ap[:, 0:n], in0=bank.ap[:, 0:n], scalar=BAND_SCALE,
                                                        in1=keep.ap[:, 0:n], op0=ALU.mult, op1=ALU.mult), "kept")
            bank.free = keep.free = [m]
            dve.wait(m, m_put)
            m = dve.do(lambda e: e.tensor_tensor_reduce(score.ap[:, 0:n], score.ap[:, 0:n], put.ap[:, 0:n], 1.0,
                                                        MASKED, ALU.add, ALU.max, sm[:, 0:1]), "score_max")
            put.free = [m]
            dve.wait(m)
            m_neg = dve.do(lambda e: e.tensor_scalar(sm[:, 1:2], sm[:, 0:1], -1.0, None, ALU.mult), "neg_max")
            p = prob.next()
            act.wait(m_neg, p.free)
            m_out = act.do(lambda e: e.activation(sm[:, 2:3], masked_col[:, :], ACT.Exp, bias=sm[:, 1:2]), "masked_prob")
            m_exp = act.do(lambda e: e.activation(p.ap[:, 0:n], score.ap[:, 0:n], ACT.Exp, bias=sm[:, 1:2],
                                                  accum_out=sm[:, 3:4]), "prob")
            score.free = [m_exp]
            dve.wait(m_out, m_exp)
            m_den = dve.do(lambda e: e.scalar_tensor_tensor(out=sm[:, 4:5], in0=sm[:, 2:3], scalar=float(SEQ - n),
                                                            in1=sm[:, 3:4], op0=ALU.mult, op1=ALU.add), "band_den")
            m_less = dve.do(lambda e: e.tensor_scalar(p.ap[:, 0:n], p.ap[:, 0:n], sm[:, 2:3], None, ALU.subtract),
                            "prob_less")
            dve.wait(m_den)
            m_r = dve.do(lambda e: e.reciprocal(sm[:, 5:6], sm[:, 4:5]), "band_rden")
            soft[t] = (p, m_less, m_r)

        def mix(t):
            k = t % TPB
            lo, hi, n, _ = window(t)
            p, m_less, m_r = soft.pop(t)
            sm = small[:, t % 2, :]
            pe.wait(m_less)
            turned = transposes(probT_bank, [p.ap[:, i * P:(i + 1) * P] for i in range(n // P)], "probT")
            p.free = [turned]
            view = Slot(probT_bank.ap[:, 0:n])
            ready = split_bank(view, turned, probT[:, 0, 0:n], probT[:, 1, 0:n], st["probT_free"], "probT")
            probT_bank.free = view.free
            pe.wait(ready, out_bank.free)
            for i in range(n // P):
                for f in products(out_bank.ap[:, :], [probT[:, h, i * P:(i + 1) * P] for h in (0, 1)],
                                  (ctx_h[:, lo + i, :], ctx_l[:, lo + i, :]), DIM, i == 0, i == n // P - 1):
                    m = pe.do(f, "mix")
            st["probT_free"] = m
            read_by[t] = m
            tot, m_tot = totals[t // TPB]
            dve.wait(m, m_tot, st["mixed"])
            m = dve.do(lambda e: e.scalar_tensor_tensor(out=mixed[:, :], in0=tot.ap[:, :], scalar=sm[:, 2:3],
                                                        in1=out_bank.ap[:, :], op0=ALU.mult, op1=ALU.add), "mixed")
            out_bank.free = [m]
            tot.free = [m]
            slot, _ = x_tile[t]
            x1 = x1_out.next()
            dve.wait(m, x1.free)
            m = dve.do(lambda e: e.scalar_tensor_tensor(out=x1.ap[:, :], in0=mixed[:, :], scalar=sm[:, 5:6],
                                                        in1=slot.ap[:, :], op0=ALU.mult, op1=ALU.add), "x1")
            st["mixed"] = m
            slot.free = [m]
            so = s_out.next()
            dve.wait(so.free)
            m_s = layer_norm(x1.ap[:, :], [x1.ap[:, :]], so.ap[:, :], m, 1, "ln")
            b, r = rows(t)
            sp.wait(m)
            x1_stored[t] = sp.do(lambda e: e.dma_start(x1_dram[b, r:r + P, :], x1.ap[:, :]), f"x1_store{t % 2}", 16)
            sp.wait(m_s)
            stream_stored[0][t] = sp.do(lambda e: e.dma_start(stream[0][b, 1 + r:1 + r + P, :], so.ap[:, :]),
                                        f"s_store{t % 2}", 16)
            x1.free = [x1_stored[t], m_s]
            so.free = [stream_stored[0][t]]

        prepare_batch(0)
        for t in range(TILES + 3):
            if t < TILES:
                load_x(t)
                prepare_ctx(t)
            if 0 <= t - 1 < TILES:
                query(t - 1)
            if 0 <= t - 3 < TILES:
                mix(t - 3)
            if 0 <= t - 2 < TILES:
                scores(t - 2)
            if t % TPB == TPB - 2 and t // TPB + 1 < BATCH:
                prepare_batch(t // TPB + 1)
            if t == 3:
                attend_ready = load_attend_weights(0, None)
        return attend_ready

    def attend_phase(l, src, dst, weights_ready, start_after):
        plan = Plan(attend_weights_end)
        sfx = f"_{l}"
        kT = plan.tensor("kT" + sfx, [P, HEADS, SEQ], F32R)
        v_rows = plan.tensor("v_rows" + sfx, [P, TPB, HEADS * HD])
        x_in = Ring([Slot(plan.tensor(f"s_in{i}" + sfx, [P, DIM + HALF])) for i in range(5)])
        hT = Ring([Slot(plan.tensor(f"hT{i}" + sfx, [P, 2, DIM], F32R)) for i in range(2)])
        square = Slot(plan.tensor("square" + sfx, [P, 2, DIM]))
        with_cos = Slot(plan.tensor("with_cos" + sfx, [P, 2, DIM]))
        with_sin = Slot(plan.tensor("with_sin" + sfx, [P, 2, DIM]))
        turned_qk = Slot(plan.tensor("turned_qk" + sfx, [P, 2, DIM]))
        qT = Ring([Slot(plan.tensor(f"qT{i}" + sfx, [P, HEADS, 2, P], F32R)) for i in range(2)])
        rope_cos = plan.tensor("rope_cos" + sfx, [P, TPB, 2 * HD])
        rope_sin = plan.tensor("rope_sin" + sfx, [P, TPB, 2 * HD])
        scales = plan.tensor("scales" + sfx, [P, 2 * HD])
        far = plan.tensor("far" + sfx, [P, WIN])
        score = Ring([Slot(plan.tensor(f"lscore{i}" + sfx, [P, WIN])) for i in range(3)])
        prob = Ring([Slot(plan.tensor(f"lprob{i}" + sfx, [P, WIN])) for i in range(3)])
        probT = Ring([Slot(plan.tensor(f"lprobT{i}" + sfx, [P, WIN])) for i in range(3)])
        o_rows = Slot(plan.tensor("o_rows" + sfx, [P, DIM]))
        oT = Slot(plan.tensor("oT" + sfx, [P, 2, DIM], F32R))
        s_out = Ring([Slot(plan.tensor(f"a_out{i}" + sfx, [P, DIM])) for i in range(2)])

        qk_banks = Slot(bank_pair)
        vy_bank = Slot(banks[0])
        turn_banks = Ring([Slot(banks[1]), Slot(banks[2])])
        score_banks = Ring([Slot(banks[3]), Slot(banks[4])])
        o_bank = Slot(banks[5])
        for q in (sp, pe, act, dve, pool):
            q.wait(start_after)

        m = [sp.do(lambda e: e.dma_start(rope_cos[:, :, :], consts["rope_cos"]), "rope_in", 16),
             sp.do(lambda e: e.dma_start(rope_sin[:, :, :], consts["rope_sin"]), "rope_in", 16),
             sp.do(lambda e: e.dma_start(scales[:, 0:HD], q_scale[l].partition_broadcast(P)), "rope_in", 16),
             sp.do(lambda e: e.dma_start(scales[:, HD:], k_scale[l].partition_broadcast(P)), "rope_in", 16),
             sp.do(lambda e: e.dma_start(far[:, :], consts["far"]), "rope_in", 16)]
        pool.wait(m[-1])
        spread = scales[:, :].unsqueeze(1).to_broadcast([P, TPB, 2 * HD])
        m_cos = pool.do(lambda e: e.tensor_tensor(rope_cos[:, :, :], rope_cos[:, :, :], spread, ALU.mult), "rope_scaled")
        m_sin = pool.do(lambda e: e.tensor_tensor(rope_sin[:, :, :], rope_sin[:, :, :], spread, ALU.mult), "rope_scaled")
        rope_ready, far_ready = [m_cos, m_sin], m[-1]
        m_zero = []
        for s in qT.slots:
            pool.wait(m_sin, m_zero)
            m_zero.append(pool.do(lambda e, s=s: e.memset(s.ap[HD:, :, 1, :].bitcast(F32), 0.0), "qT_zero"))
        pool.wait(m_zero)

        x_tile, h_slot, v_ready, qk_ready, q_slot, k_ready = {}, {}, {}, {}, {}, {}
        attended = [None] * TILES

        def load(t):
            b, r = rows(t)
            slot = x_in.next()
            sp.wait(slot.free, stream_stored[src][t], zero_rows[-1], stream_stored[src][t - 1] if t else None)
            sp.do(lambda e: e.dma_start(slot.ap[:, 0:DIM], stream[src][b, 1 + r:1 + r + P, :]), f"s_in{t % 5}", 16)
            x_tile[t] = (slot, sp.do(lambda e: e.dma_start(slot.ap[:, DIM:], stream[src][b, r:r + P, HALF:]),
                                     f"s_in{t % 5}", 16))

        def turn_h(t):
            slot, loaded = x_tile[t]
            pe.wait(loaded)
            bank = turn_banks.next()
            cols = [0, P, DIM, DIM + P]
            turned = transposes(bank, [slot.ap[:, c:c + P] for c in cols], "h_turned")
            h = hT.next()
            ready = split_bank(bank, turned, h.ap[:, 0, :], h.ap[:, 1, :], h.free, "hT")
            h_slot[t] = (h, ready)

        def project_pieces(t):
            h, ready = h_slot[t]
            pieces = []
            for part, bank in ((2, vy_bank.ap[:, :]), (0, qk_banks.ap[:, 0, :]), (1, qk_banks.ap[:, 1, :])):
                for c in range(KC):
                    cols = slice(part * DIM, (part + 1) * DIM)
                    fs = products(bank, [h.ap[:, i, c * P:(c + 1) * P] for i in (0, 1)],
                                  (wqkv_h[:, c, cols], wqkv_l[:, c, cols]), DIM, c == 0, c == KC - 1)
                    pieces += [(part, c, i, f) for i, f in enumerate(fs)]
            marks = {}

            def emit(piece):
                part, c, i, f = piece
                if (c, i) == (0, 0):
                    pe.wait(ready, weights_ready, vy_bank.free if part == 2 else qk_banks.free)
                last = (c, i) == (KC - 1, 2)
                m = pe.do(f, "projected" if last else None)
                if last:
                    marks[part] = m
                    if part == 2:
                        old = attended[t - TPB + 2] if t >= TPB else None
                        act.wait(m, old)
                        v_ready[t] = act.do(lambda e: e.activation(v_rows[:, t % TPB, :], vy_bank.ap[:, :], ACT.Copy),
                                            "v_rows")
                        vy_bank.free = [v_ready[t]]
                    if part == 1:
                        h.free = [m]
                        qk_ready[t] = [marks[0], m]
            return [lambda p=p: emit(p) for p in pieces]

        def rope_steps(t):
            k = t % TPB
            nm = norm[:, t % 2, :]
            act.wait(qk_ready[t], square.free)
            flat = lambda s: s[:, :, :].rearrange("p a n -> p (a n)")
            m_sq = act.do(lambda e: e.activation(flat(square.ap), flat(qk_banks.ap), ACT.Square), "squared")
            table = lambda s: s[:, k, :].rearrange("p (a d) -> p a d", a=2).unsqueeze(2).to_broadcast([P, 2, HEADS, HD])
            by_head = lambda s: s[:, :, :].rearrange("p a (h d) -> p a h d", h=HEADS)
            heads16 = lambda s: s[:, :, :].rearrange("p a (h d) -> p (a h) d", d=HD)
            marks = {}

            def reduce():
                dve.wait(m_sq)
                m = dve.do(lambda e: e.tensor_reduce(nm[:, 0:16], heads16(square.ap), AX, ALU.add), "norm_sum")
                square.free = [m]
                pool.wait(m)
                m = pool.do(lambda e: e.tensor_scalar(nm[:, 0:16], nm[:, 0:16], NORM_FLOOR ** 2, 0.0, ALU.max, ALU.add),
                            "norm_floor")
                pool.wait(m)
                marks["r"] = pool.do(lambda e: e.tensor_tensor(nm[:, 16:32], nm[:, 0:16], half_power[:, :], ALU.pow),
                                     "norm_inverse")

            def cos():
                dve.wait(qk_ready[t], rope_ready, with_cos.free, m_sq)
                marks["cos"] = dve.do(lambda e: e.tensor_tensor(by_head(with_cos.ap), by_head(qk_banks.ap),
                                                                table(rope_cos), ALU.mult), "with_cos")

            def sin():
                dve.wait(with_sin.free)
                marks["sin"] = dve.do(lambda e: e.tensor_tensor(by_head(with_sin.ap), by_head(qk_banks.ap),
                                                                table(rope_sin), ALU.mult), "with_sin")
                qk_banks.free = [marks["sin"]]

            def combine():
                pool.wait(marks["cos"], marks["sin"], turned_qk.free)
                h2 = HD // 2
                for a, b in ((0, h2), (h2, 0)):
                    m = pool.do(lambda e, a=a, b=b: e.tensor_tensor(
                        heads16(turned_qk.ap)[:, :, a:a + h2], heads16(with_cos.ap)[:, :, a:a + h2],
                        heads16(with_sin.ap)[:, :, b:b + h2], ALU.add), "rotated")
                with_cos.free = with_sin.free = [m]
                pool.wait(m, marks["r"])
                inv = nm[:, 16:32].unsqueeze(2).to_broadcast([P, 16, HD])
                marks["qk"] = pool.do(lambda e: e.tensor_tensor(heads16(turned_qk.ap), heads16(turned_qk.ap), inv,
                                                                ALU.mult), "qk_scaled")
            return [reduce, cos, sin, combine], marks

        def turn_qk(t, marks):
            k = t % TPB
            pe.wait(marks["qk"])
            qb, kb = turn_banks.next(), turn_banks.next()
            mq = transposes(qb, [turned_qk.ap[:, 0, i * P:(i + 1) * P] for i in range(4)], "q_turned")
            mk = transposes(kb, [turned_qk.ap[:, 1, i * P:(i + 1) * P] for i in range(4)], "k_turned")
            turned_qk.free = [mk]
            q = qT.next()
            q_slot[t] = q
            lo, hi = slice(0, HD), slice(HD, P)
            pairs = lambda bank, rows_: bank.ap[rows_, :].rearrange("p (i n) -> p i n", i=4)
            marks_q, marks_k = [], []
            act.wait(mq, q.free)
            dve.wait(mq, q.free, m_zero)
            old = attended[t - TPB + 2] if t >= TPB else None
            for odd, here in ((0, lo), (1, hi)):
                src = pairs(qb, here)
                for where in (lo, hi):
                    m = act.do(lambda e, src=src, where=where, odd=odd: e.activation(q.ap[where, odd::2, 0, :], src,
                                                                                     ACT.Copy), "qT_high")
                    marks_q.append(m)
                    if where == here:
                        own = m
                dve.wait(own, marks_q[-1])
                marks_q.append(dve.do(lambda e, src=src, here=here, odd=odd: e.tensor_tensor(
                    q.ap[lo, odd::2, 1, :], src, q.ap[here, odd::2, 0, :].bitcast(F32), ALU.subtract), "qT_low"))
            qb.free = [marks_q[-1]]
            act.wait(mk, old)
            dve.wait(mk, old)
            cols = slice(k * P, (k + 1) * P)
            for odd, here in ((0, lo), (1, hi)):
                src = pairs(kb, here)
                m = act.do(lambda e, src=src, odd=odd: e.activation(kT[lo, odd::2, cols], src, ACT.Copy), "kT_high")
                dve.wait(m)
                marks_k += [m, dve.do(lambda e, src=src, odd=odd: e.tensor_tensor(
                    kT[hi, odd::2, cols], src, kT[lo, odd::2, cols].bitcast(F32), ALU.subtract), "kT_low")]
            kb.free = [marks_k[-1]]
            q_slot[t], k_ready[t] = (q, marks_q), marks_k

        def attend(t, pieces, fillers):
            live = 0 <= t < TILES
            soft = {}
            if live:
                k = t % TPB
                w = min(k, 2) + 1
                n = w * P
                first = (k - w + 1) * P
                q, q_marks = q_slot[t]
                sm = small[:, t % 2, :]
                keys_ready = [k_ready[t - i] for i in range(w)]
            steps = HEADS + 2

            for i in range(steps):
                if live and i < HEADS:
                    bank, sc, p = score_banks.next(), score.next(), prob.next()
                    pe.wait(q_marks, keys_ready, bank.free)
                    for part in (0, 1):
                        m = pe.do(lambda e, part=part, i=i, bank=bank: e.matmul(
                            bank.ap[:, 0:n], q.ap[:, i, part, :], kT[:, i, first:first + n],
                            start=(part == 0), stop=(part == 1)), "lscores" if part else None)
                    if i == HEADS - 1:
                        q.free = [m]
                    dve.wait(m, sc.free, far_ready)
                    m = dve.do(lambda e, i=i, bank=bank, sc=sc: e.tensor_tensor_reduce(
                        sc.ap[:, 0:n], bank.ap[:, 0:n], far[:, WIN - n:], 1.0, BIG, ALU.add, ALU.min,
                        sm[:, i:i + 1]), "lmax")
                    bank.free = [m]
                    act.wait(m, p.free)
                    m = act.do(lambda e, i=i, sc=sc, p=p: e.activation(
                        p.ap[:, 0:n], sc.ap[:, 0:n], ACT.Exp, bias=sm[:, i:i + 1], scale=-1.0,
                        accum_out=sm[:, 8 + i:9 + i]), "lprob")
                    sc.free = [m]
                    soft[i] = (p, m)
                for f in pieces[len(pieces) * i // steps: len(pieces) * (i + 1) // steps]:
                    f()
                if live and 1 <= i <= HEADS:
                    p, m = soft[i - 1]
                    pe.wait(m)
                    bank, pt = turn_banks.next(), probT.next()
                    turned = transposes(bank, [p.ap[:, j * P:(j + 1) * P] for j in range(w)], "lprobT")
                    p.free = [turned]
                    eng = act if i % 2 else dve
                    eng.wait(turned, pt.free)
                    if eng is act:
                        m = act.do(lambda e, bank=bank, pt=pt: e.activation(pt.ap[:, 0:n], bank.ap[:, 0:n], ACT.Copy),
                                   "lprobT_a")
                    else:
                        m = dve.do(lambda e, bank=bank, pt=pt: e.tensor_copy(pt.ap[:, 0:n], bank.ap[:, 0:n]),
                                   "lprobT_v")
                    bank.free = [m]
                    soft[i - 1] = (pt, m)
                if i < len(fillers):
                    fillers[i]()
                if live and i >= 2:
                    h = i - 2
                    pt, m = soft[h]
                    pe.wait(m, [v_ready[t - j] for j in range(w)], o_bank.free)
                    for j in range(w):
                        m = pe.do(lambda e, j=j, h=h, pt=pt: e.matmul(
                            o_bank.ap[:, h * HD:(h + 1) * HD], pt.ap[:, j * P:(j + 1) * P],
                            v_rows[:, k - w + 1 + j, h * HD:(h + 1) * HD], start=(h == 0 and j == 0),
                            stop=(j == w - 1), skip_group_check=True), "lmix" if j == w - 1 else None)
                    pt.free = [m]
            if not live:
                return
            attended[t] = m
            m_den = soft and act.signals("lprob")
            dve.wait((m_den, m_den.value))
            m_r = dve.do(lambda e: e.reciprocal(sm[:, 16:24], sm[:, 8:16]), "lrden")
            dve.wait(m_r, m, o_rows.free)
            m = dve.do(lambda e: e.tensor_tensor(
                o_rows.ap[:, :].rearrange("p (h d) -> p h d", h=HEADS),
                o_bank.ap[:, :].rearrange("p (h d) -> p h d", h=HEADS),
                sm[:, 16:24].unsqueeze(2).to_broadcast([P, HEADS, HD]), ALU.mult), "o_rows")
            o_bank.free = [m]
            pe.wait(m)
            bank = turn_banks.next()
            turned = transposes(bank, [o_rows.ap[:, c * P:(c + 1) * P] for c in range(KC)], "o_turned")
            o_rows.free = [turned]
            ready = split_bank(bank, turned, oT.ap[:, 0, :], oT.ap[:, 1, :], oT.free, "oT")
            pe.wait(ready, weights_ready, vy_bank.free)
            for c in range(KC):
                for f in products(vy_bank.ap[:, :], [oT.ap[:, i2, c * P:(c + 1) * P] for i2 in (0, 1)],
                                  (wo_h[:, c, :], wo_l[:, c, :]), DIM, c == 0, c == KC - 1):
                    m = pe.do(f, "wo_done")
            oT.free = [m]
            slot, _ = x_tile[t]
            so = s_out.next()
            dve.wait(m, so.free)
            m = dve.do(lambda e: e.tensor_tensor(so.ap[:, :], vy_bank.ap[:, :], slot.ap[:, 0:DIM], ALU.add), "a_out")
            vy_bank.free = [m]
            slot.free = [m]
            b, r = rows(t)
            sp.wait(m)
            stream_stored[dst][t] = sp.do(lambda e: e.dma_start(stream[dst][b, 1 + r:1 + r + P, :], so.ap[:, :]),
                                          f"a_store{t % 2}", 16)
            so.free = [stream_stored[dst][t]]

        load(0)
        load(1)
        for t in range(TILES + 2):
            if t + 2 < TILES:
                load(t + 2)
            fillers, marks = [], None
            if t < TILES:
                turn_h(t)
            if 1 <= t <= TILES:
                fillers, marks = rope_steps(t - 1)
            attend(t - 2, project_pieces(t) if t < TILES else [], fillers)
            if marks:
                turn_qk(t - 1, marks)

    def ffn_phase(l, src, dst, start_after):
        plan = Plan(phase_base)
        sfx = f"_f{l}"
        w1_h, w1_raw = plan.pair("w1_h" + sfx, [P, KC, 2 * HID])
        w1_l = plan.tensor("w1_l" + sfx, [P, KC, 2 * HID], F32R)
        w2_h, w2_raw = plan.pair("w2_h" + sfx, [P, HC, DIM])
        w2_l = plan.tensor("w2_l" + sfx, [P, HC, DIM], F32R)
        hT = Ring([Slot(plan.tensor(f"fhT{i}" + sfx, [P, 2, KC, GROUP * P], F32R)) for i in range(2)])
        uT = Ring([Slot(plan.tensor(f"uT{i}" + sfx, [P, 2, GROUP * P], F32R)) for i in range(3)])
        gate = Ring([Slot(plan.tensor(f"gate{i}" + sfx, [P, GROUP * P])) for i in range(2)])
        u = Ring([Slot(plan.tensor(f"u{i}" + sfx, [P, GROUP * P])) for i in range(2)])
        gain = plan.tensor("gain" + sfx, [P, DIM])
        shift = plan.tensor("shift" + sfx, [P, DIM])
        bias2 = plan.tensor("bias2" + sfx, [P, DIM])
        bias1 = plan.tensor("bias1" + sfx, [P, 2, HC])
        h_in = Ring([Slot(plan.tensor(f"h_in{i}" + sfx, [P, DIM])) for i in range(2)])
        h_norm = Ring([Slot(plan.tensor(f"h_norm{i}" + sfx, [P, DIM])) for i in range(2)])
        res = Ring([Slot(plan.tensor(f"res{i}" + sfx, [P, DIM])) for i in range(3)])
        add_x1 = l == DEPTH - 1
        x1_in = Ring([Slot(plan.tensor(f"x1_in{i}" + sfx, [P, DIM])) for i in range(1)]) if add_x1 else None

        y_banks = [Slot(bank_pair[:, 0, :]), Slot(bank_pair[:, 1, :]), Slot(banks[0][:, :]), Slot(banks[1][:, :])]
        h_banks = Ring([Slot(banks[2]), Slot(banks[3]), Slot(banks[4])])
        turn_bank = Slot(banks[5])
        for q in (sp, pe, act, dve, pool):
            q.wait(start_after)

        for i, (dst_ap, src_ap) in enumerate(((gain[:, :], ln_g[l].partition_broadcast(P)),
                                              (shift[:, :], ln_b[l].partition_broadcast(P)),
                                              (bias2[:, :], b2[l].partition_broadcast(P)))):
            sp.do(lambda e, d=dst_ap, s=src_ap: e.dma_start(d, s), "ffn_vectors", 16)
        full = HC - 1
        for half in (0, 1):
            v = b1[l, half * HID:(half + 1) * HID]
            sp.do(lambda e, v=v, half=half: e.dma_start(bias1[:, half, 0:full],
                                                        v[0:full * P].rearrange("(j p) -> p j", p=P)), "ffn_vectors", 16)
            vectors = sp.do(lambda e, v=v, half=half: e.dma_start(bias1[0:hid_rows(full), half, full:HC],
                                                                  v[full * P:HID].unsqueeze(1)), "ffn_vectors", 16)
        w1v = w1[l].rearrange("(c p) n -> p c n", p=P)
        w1_ready, w2_ready = {}, {}
        chunks = [(0, 1), (1, 2), (2, 4), (4, 7), (7, HC)]

        def load_weights(i):
            a, b = chunks[i]
            pieces = []
            for half in (0, 1):
                cols = slice(half * HID + a * P, half * HID + min(b * P, HID))
                loaded = sp.do(lambda e, cols=cols: e.dma_start(w1_raw[:, :, cols], w1v[:, :, cols]), f"w1_in{i}", 16)
                pieces.append((cols, loaded))
            for cols, _ in pieces:
                m = split_weight(dve, w1_h[:, :, cols], w1_l[:, :, cols], w1_raw[:, :, cols], loaded, "weight")
            for j in range(a, b):
                w1_ready[j] = m
            whole = min(b, full)
            if whole > a:
                loaded = sp.do(lambda e: e.dma_start(w2_raw[:, a:whole, :], w2[l, a * P:whole * P].rearrange(
                    "(j p) n -> p j n", p=P)), f"w2_in{i}", 16)
                m = split_weight(dve, w2_h[:, a:whole, :], w2_l[:, a:whole, :], w2_raw[:, a:whole, :], loaded, "weight")
                for j in range(a, whole):
                    w2_ready[j] = m
            if b == HC:
                r = hid_rows(full)
                loaded = sp.do(lambda e: e.dma_start(w2_raw[0:r, full, :], w2[l, full * P:HID]), "w2_tail_in", 16)
                w2_ready[full] = split_weight(dve, w2_h[0:r, full, :], w2_l[0:r, full, :], w2_raw[0:r, full, :],
                                              loaded, "weight")

        h_slots, h_marks = {}, {}

        def normalise(t):
            b, r = rows(t)
            g, i = divmod(t, GROUP)
            slot, hn = h_in.next(), h_norm.next()
            sp.wait(slot.free, stream_stored[src][t], zero_rows[-1], stream_stored[src][t - 1] if t else None)
            sp.do(lambda e: e.dma_start(slot.ap[:, 0:HALF], stream[src][b, 1 + r:1 + r + P, 0:HALF]), f"h_in{t % 2}", 16)
            loaded = sp.do(lambda e: e.dma_start(slot.ap[:, HALF:], stream[src][b, r:r + P, HALF:]), f"h_in{t % 2}", 16)
            dve.wait(hn.free)
            m = layer_norm(slot.ap[:, :], [slot.ap[:, :]], hn.ap[:, :], loaded, t % 2, "ln")
            slot.free = [m]
            pool.wait(m, vectors)
            m = pool.do(lambda e: e.tensor_tensor(hn.ap[:, :], hn.ap[:, :], gain[:, :], ALU.mult), "gained")
            pool.wait(m)
            m = pool.do(lambda e: e.tensor_tensor(hn.ap[:, :], hn.ap[:, :], shift[:, :], ALU.add), "shifted")
            pe.wait(m)
            turned = transposes(turn_bank, [hn.ap[:, c * P:(c + 1) * P] for c in range(KC)], "fh_turned")
            hn.free = [turned]
            if i == 0:
                h_slots[g], h_marks[g] = hT.next(), []
            h = h_slots[g]
            view = Slot(turn_bank.ap[:, :].rearrange("p (c n) -> p c n", c=KC))
            h_marks[g] += split_bank(view, turned, h.ap[:, 0, :, i * P:(i + 1) * P], h.ap[:, 1, :, i * P:(i + 1) * P],
                                     h.free, "fhT")
            turn_bank.free = view.free

        def up(g, j):
            n = hid_rows(j)
            h = h_slots[g]
            marks, bank_of = {}, {}
            for half in (1, 0):
                bank = h_banks.next()
                bank_of[half] = bank
                cols = slice(half * HID + j * P, half * HID + j * P + n)
                pe.wait(h_marks[g], w1_ready[j], bank.free)
                for c in range(KC):
                    fs = [lambda e, a=a, b=b, s=s, p=p, bank=bank: e.matmul(bank.ap[0:n, :], a, b, start=s, stop=p)
                          for a, b, s, p in ((w1_h[:, c, cols], h.ap[:, 0, c, :], c == 0, False),
                                             (w1_h[:, c, cols], h.ap[:, 1, c, :], False, False),
                                             (w1_l[:, c, cols], h.ap[:, 0, c, :], False, c == KC - 1))]
                    for f in fs:
                        m = pe.do(f, "up")
                marks[half] = m
            if j == HC - 1:
                h.free = [m]
            gt, uu, ut = gate.next(), u.next(), uT.next()
            act.wait(marks[1], gt.free, vectors)
            m = act.do(lambda e: e.activation(gt.ap[0:n, :], bank_of[1].ap[0:n, :], ACT.Gelu,
                                              bias=bias1[0:n, 1, j:j + 1]), "gate")
            bank_of[1].free = [m]
            dve.wait(m, marks[0], uu.free, vectors)
            m = dve.do(lambda e: e.scalar_tensor_tensor(out=uu.ap[0:n, :], in0=bank_of[0].ap[0:n, :],
                                                        scalar=bias1[0:n, 0, j:j + 1], in1=gt.ap[0:n, :],
                                                        op0=ALU.add, op1=ALU.mult), "u")
            bank_of[0].free = gt.free = [m]
            act.wait(m, ut.free)
            m_h = act.do(lambda e: e.activation(ut.ap[0:n, 0, :], uu.ap[0:n, :], ACT.Copy), "uT_high")
            dve.wait(m_h, ut.free)
            m_l = dve.do(lambda e: e.tensor_tensor(ut.ap[0:n, 1, :], uu.ap[0:n, :], ut.ap[0:n, 0, :].bitcast(F32),
                                                   ALU.subtract), "uT_low")
            uu.free = [m_l]
            return ut, [m_h, m_l]

        def down(j, ut, ready):
            n = hid_rows(j)
            pe.wait(ready, w2_ready[j])
            marks = []
            for i in range(GROUP):
                if j == 0:
                    pe.wait(y_banks[i].free)
                for f in products(y_banks[i].ap, [ut.ap[0:n, h, i * P:(i + 1) * P] for h in (0, 1)],
                                  (w2_h[0:n, j, :], w2_l[0:n, j, :]), DIM, j == 0, j == HC - 1):
                    m = pe.do(f, "down")
                marks.append(m)
            ut.free = [m]
            return marks

        def finish(g, i, m_y):
            t = g * GROUP + i
            b, r = rows(t)
            slot = res.next()
            sp.wait(slot.free)
            loaded = sp.do(lambda e: e.dma_start(slot.ap[:, :], stream[src][b, 1 + r:1 + r + P, :]), f"res_in{t % 3}", 16)
            pool.wait(loaded, vectors)
            m = pool.do(lambda e: e.tensor_tensor(slot.ap[:, :], slot.ap[:, :], bias2[:, :], ALU.add), "res_bias")
            if add_x1:
                xs = x1_in.next()
                sp.wait(xs.free, x1_stored[t])
                loaded = sp.do(lambda e: e.dma_start(xs.ap[:, :], x1_dram[b, r:r + P, :]), "x1_in", 16)
                pool.wait(loaded, m)
                m = pool.do(lambda e: e.tensor_tensor(slot.ap[:, :], slot.ap[:, :], xs.ap[:, :], ALU.add), "res_x1")
                xs.free = [m]
            dve.wait(m, m_y)
            m = dve.do(lambda e: e.tensor_tensor(slot.ap[:, :], y_banks[i].ap, slot.ap[:, :], ALU.add), "f_out")
            y_banks[i].free = [m]
            sp.wait(m)
            target = out[b, r:r + P, :] if add_x1 else stream[dst][b, 1 + r:1 + r + P, :]
            m = sp.do(lambda e: e.dma_start(target, slot.ap[:, :]), f"f_store{t % 3}", 16)
            slot.free = [m]
            if not add_x1:
                stream_stored[dst][t] = m
            return m

        for t in range(GROUP):
            normalise(t)
            if t == 0:
                load_weights(0)
        last = []
        for g in range(GROUPS):
            pending = None
            for j in range(HC):
                ut, ready = up(g, j)
                if g == 0 and j + 1 < len(chunks):
                    load_weights(j + 1)
                if pending:
                    down(*pending)
                pending = (j, ut, ready)
                if g + 1 < GROUPS and j in (2, 4, 6, 8):
                    normalise((g + 1) * GROUP + (j - 2) // 2)
            marks = down(*pending)
            last = [finish(g, i, marks[i]) for i in range(GROUP)]
        return last

    def everything():
        return [(s, s.value) for s in signals.values()]

    ready = band_phase()
    for l in range(DEPTH):
        after = everything()
        if l:
            ready = load_attend_weights(l, after)
        attend_phase(l, 2 * l, 2 * l + 1, ready, after)
        ffn_phase(l, 2 * l + 1, 2 * l + 2, everything())
    sp.wait(everything())

    with nc.allow_non_contiguous_dma(reason="bias columns"), nc.Block() as block:
        block.sync(sp.run)
        block.tensor(pe.run)
        block.scalar(act.run)
        block.vector(dve.run)
        block.gpsimd(pool.run)


def shape_constants():
    f = np.float32
    i, j = np.arange(P)[:, None], np.arange(WIN)[None, :]
    band01 = (np.abs(i - (j - P)) <= P).astype(f)
    back = i - (j - 2 * P)
    far = np.where((back < 0) | (back > 2 * P), f(BIG), f(0)).astype(f)
    half_idx = np.arange(0, HD, 2, dtype=f)
    inv_freq = f(1.0) / f(10000.0) ** (half_idx / f(HD))
    t = np.arange(SEQ, dtype=f)
    freqs = t[:, None] * inv_freq[None, :]
    base = (half_idx + f(0.4 * HD)) / f(1.4 * HD)
    power = (t - f(SEQ // 2)) / f(128.0)
    scale = base[None, :] ** power[:, None]
    cos, sin = np.cos(freqs), np.sin(freqs)
    c, s = [], []
    for sc, m in ((scale, -QK_SCALE), (f(1.0) / scale, 1.0)):
        c += [cos * sc * f(m), cos * sc * f(m)]
        s += [sin * sc * f(m), -sin * sc * f(m)]
    tile = lambda parts: np.ascontiguousarray(
        np.concatenate(parts, 1).astype(f).reshape(TPB, P, 2 * HD).transpose(1, 0, 2))
    return {"ident": np.eye(P, dtype=f), "zeros": np.zeros((BATCH, DIM), f), "band01": band01, "far": far,
            "rope_cos": tile(c), "rope_sin": tile(s)}


_INS = ["x", "ctx_1024", "mask_BxS2_bf1", "L0_ffn_wqkv", "L0_ffn_q_scale", "L0_ffn_k_scale", "L0_ffn_wo",
        "L0_ffn_ln_g", "L0_ffn_ln_b", "L0_ffn_w1", "L0_ffn_b1", "L0_ffn_w2", "L0_ffn_b2"]


def kernel(**inputs):
    import concourse.bacc as bacc
    from concourse.bass_utils import run_bass_kernel_spmd

    nc = bacc.Bacc("TRN2", target_bir_lowering=False, num_devices=1)
    arrays = {}

    def declare(name, a):
        a = np.ascontiguousarray(a)
        if a.dtype.kind == "b":
            a = a.view(np.uint8)
        arrays[name] = a
        return nc.dram_tensor(name, a.shape, mybir.dt.from_np(a.dtype), kind="ExternalInput").ap()

    args = [declare(f"in_{name}", inputs[name]) for name in _INS]
    consts = {name: declare(f"const_{name}", a) for name, a in shape_constants().items()}
    out = nc.dram_tensor("out_0", (BATCH, SEQ, DIM), F32, kind="ExternalOutput").ap()
    build(nc, *args, consts, out)
    r = run_bass_kernel_spmd(nc, [arrays], core_ids=[0])
    return r.results[0]["out_0"]
```

```python
import numpy as np
import concourse.bass as bass
from concourse import mybir
from concourse.alu_op_type import AluOpType as ALU

F32 = mybir.dt.float32
F32R = mybir.dt.float32r
U8 = mybir.dt.uint8
ACT = mybir.ActivationFunctionType
AX = mybir.AxisListType.X

P = 128
BATCH, SEQ, DIM = 4, 1024, 512
TPB = SEQ // P
TILES = BATCH * TPB
HALF = DIM // 2
KC = DIM // P
HEADS, HD = 8, 64
QKV = 3 * HEADS * HD
HID = int(DIM * 4 * 2 / 3)
DEPTH = 2
HC = (HID + P - 1) // P
GROUP = 4
GROUPS = TILES // GROUP
QK_SCALE = 8.0
EPS = 1e-5
NORM_FLOOR = 1e-12
MASKED = -1e9
BIG = 3.0e38
BAND_SCALE = float(np.float32(1.0) / np.sqrt(np.float32(DIM)))
WIN = 3 * P
FREE_BASE = 16512


def hid_rows(j):
    return min(P, HID - j * P)


class Signal:

    def __init__(self, sem):
        self.sem, self.value = sem, 0


class Queue:

    def __init__(self, signals):
        self.steps, self.passed, self.signals = [], {}, signals

    def wait(self, *marks):
        for mark in marks:
            if mark is None:
                continue
            if isinstance(mark, list):
                self.wait(*mark)
                continue
            signal, value = mark
            if self.passed.get(signal, 0) < value:
                self.passed[signal] = value
                self.steps.append(("wait", signal.sem, value))

    def do(self, build, signal=None, by=1):
        if signal is None:
            self.steps.append(("do", build, None, 0))
            return None
        s = self.signals(signal)
        s.value += by
        self.steps.append(("do", build, s.sem, by))
        return (s, s.value)

    def run(self, engine):
        for kind, what, *rest in self.steps:
            if kind == "wait":
                engine.wait_ge(what, rest[0])
            else:
                ins = what(engine)
                if rest[0] is not None:
                    ins.then_inc(rest[0], rest[1])


class Slot:

    def __init__(self, ap):
        self.ap, self.free = ap, []


class Ring:
    def __init__(self, slots):
        self.slots, self.n = slots, 0

    def next(self):
        self.n += 1
        return self.slots[(self.n - 1) % len(self.slots)]


def build(nc, x, ctx, mask, wqkv, q_scale, k_scale, wo, ln_g, ln_b, w1, b1, w2, b2, consts, out):
    signals = {}

    def signal(name):
        if name not in signals:
            signals[name] = Signal(nc.alloc_semaphore(name))
        return signals[name]

    sp, pe, act, dve, pool = (Queue(signal) for _ in range(5))

    class Plan:

        def __init__(self, start):
            self.at = start

        def tensor(self, name, shape, dtype=F32):
            size = int(np.prod(shape[1:])) * (1 if dtype == U8 else 4)
            t = nc.alloc_sbuf_tensor_at(name, shape, dtype, offset=self.at)
            self.at += (size + 31) // 32 * 32
            return t

        def pair(self, name, shape):
            at = self.at
            t = self.tensor(name, shape, F32R)
            raw = nc.alloc_sbuf_tensor_at(name + "_raw", shape, F32, offset=at)
            return t, raw

    fixed = Plan(FREE_BASE)
    ident = fixed.tensor("ident", [P, P])
    half_power = fixed.tensor("half_power", [P, 16])
    masked_col = fixed.tensor("masked_col", [P, 1])
    stats = fixed.tensor("stats", [P, 2, 32])
    small = fixed.tensor("small", [P, 4, 32])
    norm = fixed.tensor("norm", [P, 2, 32])
    phase_base = fixed.at

    bank_pair = nc.alloc_psum_tensor("bank_pair", [P, 2, 512], F32)[:, :, :]
    banks = [nc.alloc_psum_tensor(f"bank{i}", [P, 512], F32)[:, :] for i in range(6)]

    x1_dram = nc.dram_tensor("x1_dram", [BATCH, SEQ, DIM], F32).ap()
    stream = [nc.dram_tensor(f"stream{i}", [BATCH, SEQ + 1, DIM], F32).ap() for i in range(2 * DEPTH)]
    zero_rows = [sp.do(lambda e, s=s: e.dma_start(s[:, 0, :], consts["zeros"]), "zero_rows", 16)
                 for s in stream]
    x1_stored = [None] * TILES
    stream_stored = [[None] * TILES for _ in stream]

    def rows(t):
        return t // TPB, (t % TPB) * P

    m_ident = sp.do(lambda e: e.dma_start(ident[:, :], consts["ident"]), "ident_in", 16)
    m_half = pool.do(lambda e: e.memset(half_power[:, :], -0.5), "half_power")
    m_masked = pool.do(lambda e: e.memset(masked_col[:, :], MASKED), "masked_col")
    pool.wait(m_half)
    act.wait(m_masked)
    pe.wait(m_ident)

    def split_weight(queue_sub, h, l, raw, loaded, name):
        act.wait(loaded)
        rounded = act.do(lambda e: e.activation(l, raw, ACT.Copy), name + "_round")
        dve.wait(rounded)
        low = dve.do(lambda e: e.tensor_tensor(l, raw, l.bitcast(F32), ALU.subtract), name + "_low")
        act.wait(low)
        return act.do(lambda e: e.activation(h, raw, ACT.Copy), name + "_high")

    def transposes(bank, sources, name):
        pe.wait(bank.free)
        for i, src in enumerate(sources):
            r = lambda e, i=i, src=src: e.transpose(bank.ap[:, i * P:(i + 1) * P], src, ident[:, :])
            mark = pe.do(r, name if i == len(sources) - 1 else None)
        return mark

    def split_bank(bank, turned, high, low, free, name):
        act.wait(turned, free)
        m_high = act.do(lambda e: e.activation(high, bank.ap, ACT.Copy), name + "_high")
        dve.wait(m_high, turned, free)
        m_low = dve.do(lambda e: e.tensor_tensor(low, bank.ap, high.bitcast(F32), ALU.subtract), name + "_low")
        bank.free = [m_low]
        return [m_high, m_low]

    def products(bank, lhs, rhs, n, first=True, last=True):
        out_ap = bank
        return [lambda e, a=a, b=b, s=s, p=p: e.matmul(out_ap, a, b, start=s, stop=p)
                for a, b, s, p in ((lhs[0], rhs[0], first, False), (lhs[1], rhs[0], False, False),
                                   (lhs[0], rhs[1], False, last))]

    def layer_norm(src, pieces, dst, ready, k, name):
        st = stats[:, k, :]
        dve.wait(ready)
        for i, piece in enumerate(pieces):
            m = dve.do(lambda e, i=i, piece=piece: e.bn_stats(st[:, 6 * i:6 * i + 6], piece), name + "_stats")
        dve.wait(m)
        m = dve.do(lambda e: e.bn_aggr(st[:, 12:14], st[:, 0:6 * len(pieces)]), name + "_moments")
        pool.wait(m)
        m = pool.do(lambda e: e.tensor_scalar(st[:, 14:15], st[:, 13:14], 1.0, EPS, ALU.mult, ALU.add), name + "_var")
        pool.wait(m)
        m = pool.do(lambda e: e.tensor_tensor(st[:, 15:16], st[:, 14:15], half_power[:, 0:1], ALU.pow), name + "_rstd")
        dve.wait(m)
        return dve.do(lambda e: e.tensor_scalar(dst, src, st[:, 12:13], st[:, 15:16], ALU.subtract, ALU.mult),
                      name + "_normed")

    attend_plan = Plan(phase_base)
    wqkv_h, wqkv_raw = attend_plan.pair("wqkv_h", [P, KC, QKV])
    wqkv_l = attend_plan.tensor("wqkv_l", [P, KC, QKV], F32R)
    wo_h, wo_raw = attend_plan.pair("wo_h", [P, KC, DIM])
    wo_l = attend_plan.tensor("wo_l", [P, KC, DIM], F32R)
    attend_weights_end = attend_plan.at

    def load_attend_weights(l, free):
        ready = []
        sp.wait(free)
        act.wait(free)
        wq = wqkv[l].rearrange("(c p) n -> p c n", p=P)
        for part in (2, 0, 1):
            cols = slice(part * DIM, (part + 1) * DIM)
            loaded = sp.do(lambda e, cols=cols: e.dma_start(wqkv_raw[:, :, cols], wq[:, :, cols]), f"wqkv_in{part}", 16)
            ready.append(split_weight(dve, wqkv_h[:, :, cols], wqkv_l[:, :, cols], wqkv_raw[:, :, cols], loaded, "weight"))
        loaded = sp.do(lambda e: e.dma_start(wo_raw[:, :, :], wo[l].rearrange("(c p) n -> p c n", p=P)), "wo_in", 16)
        ready.append(split_weight(dve, wo_h[:, :, :], wo_l[:, :, :], wo_raw[:, :, :], loaded, "weight"))
        return ready

    def band_phase():
        plan = Plan(attend_weights_end)
        ctx_h = plan.tensor("ctx_h", [P, TPB, DIM], F32R)
        ctx_l = plan.tensor("ctx_l", [P, TPB, DIM], F32R)
        keyT_h = plan.tensor("keyT_h", [P, KC, SEQ], F32R)
        keyT_l = plan.tensor("keyT_l", [P, KC, SEQ], F32R)
        ctx_in = Ring([Slot(plan.tensor(f"ctx_in{i}", [P, DIM])) for i in range(3)])
        sum_in = Ring([Slot(plan.tensor(f"sum_in{i}", [P, DIM])) for i in range(2)])
        x_in = Ring([Slot(plan.tensor(f"x_in{i}", [P, DIM])) for i in range(7)])
        xn = Ring([Slot(plan.tensor(f"xn{i}", [P, DIM])) for i in range(2)])
        queryT = Ring([Slot(plan.tensor(f"queryT{i}", [P, 2, DIM], F32R)) for i in range(2)])
        ctx_sum = Slot(plan.tensor("ctx_sum", [P, DIM]))
        total = Ring([Slot(plan.tensor(f"ctx_total{i}", [P, DIM])) for i in range(2)])
        ones = plan.tensor("ones", [P, P])
        band01 = plan.tensor("band01", [P, WIN])
        key_mask = Slot(plan.tensor("key_mask", [P, SEQ], U8))
        key01 = Slot(plan.tensor("key01", [P, SEQ]))
        keep = Ring([Slot(plan.tensor(f"keep{i}", [P, WIN])) for i in range(2)])
        put = Ring([Slot(plan.tensor(f"put{i}", [P, WIN])) for i in range(2)])
        score = Slot(plan.tensor("score", [P, WIN]))
        prob = Ring([Slot(plan.tensor(f"prob{i}", [P, WIN])) for i in range(2)])
        probT = Ring([Slot(plan.tensor(f"probT{i}", [P, 2, WIN], F32R)) for i in range(2)])
        mixed = Slot(plan.tensor("mixed", [P, DIM]))
        x1_out = Ring([Slot(plan.tensor(f"x1_out{i}", [P, DIM])) for i in range(2)])
        s_out = Ring([Slot(plan.tensor(f"s_out{i}", [P, DIM])) for i in range(2)])
        soft = plan.tensor("soft", [P, 8, 8])
        moments = plan.tensor("moments", [P, 8, 16])

        turn_banks = Ring([Slot(banks[0]), Slot(banks[1])])
        score_bank = Ring([Slot(banks[2]), Slot(banks[3])])
        probT_bank = Slot(banks[4])
        out_bank = Ring([Slot(banks[5]), Slot(bank_pair[:, 1, :])])
        total_bank = Slot(bank_pair[:, 0, :])

        m_ones = pool.do(lambda e: e.memset(ones[:, :], 1.0), "ones")
        m_band = sp.do(lambda e: e.dma_start(band01[:, :], consts["band01"]), "band01_in", 16)
        ctx_ready, read_by = [None] * TILES, [None] * TILES
        x_tile, x_normed, ctx_tile, sums, q_ready, masks, scored, totals, x1_tile, mixes = ({} for _ in range(10))
        probs, probTs = {}, {}
        key_state = {}

        def load(t):
            b, r = rows(t)
            slot = x_in.next()
            sp.wait(slot.free)
            x_tile[t] = (slot, sp.do(lambda e: e.dma_start(slot.ap[:, :], x[b, r:r + P, :]), f"x_in{t % 7}", 16))
            kslot = ctx_in.next()
            sp.wait(kslot.free)
            ctx_tile[t] = (kslot, sp.do(lambda e: e.dma_start(kslot.ap[:, :], ctx[b, r:r + P, :]), f"ctx_in{t % 3}", 16))

        def add_to_sum(t):
            b, r = rows(t)
            slot = sum_in.next()
            sp.wait(slot.free)
            loaded = sp.do(lambda e: e.dma_start(slot.ap[:, :], ctx[b, r:r + P, :]), f"sum_in{t % 2}", 16)
            pool.wait(loaded)
            if r == 0:
                pool.wait(ctx_sum.free)
                m = pool.do(lambda e: e.tensor_scalar(ctx_sum.ap[:, :], slot.ap[:, :], 1.0, 0.0, ALU.mult, ALU.add),
                            "ctx_sum")
            else:
                pool.wait(sums["last"])
                m = pool.do(lambda e: e.tensor_tensor(ctx_sum.ap[:, :], ctx_sum.ap[:, :], slot.ap[:, :], ALU.add),
                            "ctx_sum")
            sums["last"] = m
            slot.free = [m]
            if t % TPB == TPB - 1:
                pe.wait(m, m_ones, total_bank.free)
                m = pe.do(lambda e: e.matmul(total_bank.ap, ones[:, :], ctx_sum.ap[:, :], start=True, stop=True), "total")
                ctx_sum.free = [m]
                tot = total.next()
                act.wait(m, tot.free)
                m = act.do(lambda e: e.activation(tot.ap[:, :], total_bank.ap, ACT.Copy), "total_out")
                total_bank.free = [m]
                totals[b] = (tot, m)

        def prepare_ctx(t):
            slot, loaded = ctx_tile[t]
            k = t % TPB
            pe.wait(loaded)
            bank = turn_banks.next()
            turned = transposes(bank, [slot.ap[:, c * P:(c + 1) * P] for c in range(KC)], "ctx_turned")
            old = [read_by[t - TPB + 1]] if t >= TPB else []
            view = Slot(bank.ap[:, :].rearrange("p (c n) -> p c n", c=KC))
            key_marks = split_bank(view, turned, keyT_h[:, :, k * P:(k + 1) * P], keyT_l[:, :, k * P:(k + 1) * P],
                                   old, "keyT")
            bank.free = view.free
            act.wait(loaded)
            m_h = act.do(lambda e: e.activation(ctx_h[:, k, :], slot.ap[:, :], ACT.Copy), "ctx_high")
            pool.wait(m_h)
            m_l = pool.do(lambda e: e.tensor_tensor(ctx_l[:, k, :], slot.ap[:, :], ctx_h[:, k, :].bitcast(F32),
                                                    ALU.subtract), "ctx_low")
            slot.free = [turned, m_h, m_l]
            ctx_ready[t] = key_marks + [m_h, m_l]

        def statistics(src, ready, st):
            dve.wait(ready)
            m = dve.do(lambda e: e.bn_stats(st[:, 0:6], src), "ln_stats")
            dve.wait(m)
            m = dve.do(lambda e: e.bn_aggr(st[:, 12:14], st[:, 0:6]), "ln_moments")
            pool.wait(m)
            m = pool.do(lambda e: e.tensor_scalar(st[:, 14:15], st[:, 13:14], 1.0, EPS, ALU.mult, ALU.add), "ln_var")
            pool.wait(m)
            return pool.do(lambda e: e.tensor_tensor(st[:, 15:16], st[:, 14:15], half_power[:, 0:1], ALU.pow), "ln_rstd")

        def normalise(src, dst, st, ready):
            dve.wait(ready)
            return dve.do(lambda e: e.tensor_scalar(dst, src, st[:, 12:13], st[:, 15:16], ALU.subtract, ALU.mult),
                          "ln_normed")

        def query_statistics(t):
            slot, loaded = x_tile[t]
            x_normed[t] = statistics(slot.ap[:, :], loaded, moments[:, t % 4, :])

        def normalise_query(t):
            slot, _ = x_tile[t]
            n = xn.next()
            x_normed[t] = (n, normalise(slot.ap[:, :], n.ap[:, :], moments[:, t % 4, :], [x_normed[t], n.free]))

        def turn_query(t):
            n, m = x_normed.pop(t)
            pe.wait(m)
            bank = turn_banks.next()
            turned = transposes(bank, [n.ap[:, c * P:(c + 1) * P] for c in range(KC)], "x_turned")
            n.free = [turned]
            q = queryT.next()
            q_ready[t] = (q, split_bank(bank, turned, q.ap[:, 0, :], q.ap[:, 1, :], q.free, "queryT"))

        def window(t):
            k = t % TPB
            lo, hi = max(k - 1, 0), min(k + 1, TPB - 1)
            return lo, hi, (hi - lo + 1) * P, (lo - (k - 1)) * P

        def make_masks(t):
            lo, _, n, off = window(t)
            b, r = rows(t)
            if r == 0:
                sp.wait(key_mask.free)
                loaded = sp.do(lambda e: e.dma_start(key_mask.ap[:, :], mask[b].partition_broadcast(P)), "mask_in", 16)
                pool.wait(loaded, key01.free)
                key_state["ready"] = pool.do(lambda e: e.tensor_scalar(key01.ap[:, :], key_mask.ap[:, :], 1.0, 0.0,
                                                                       ALU.mult, ALU.add), "key01")
                key_mask.free = [key_state["ready"]]
            kp, pt = keep.next(), put.next()
            pool.wait(key_state["ready"], m_band, kp.free)
            m_keep = pool.do(lambda e: e.tensor_tensor(kp.ap[:, 0:n], band01[:, off:off + n],
                                                       key01.ap[:, lo * P:lo * P + n], ALU.mult), "keep")
            key01.free = [m_keep]
            pool.wait(m_keep, pt.free)
            m_put = pool.do(lambda e: e.tensor_scalar(pt.ap[:, 0:n], kp.ap[:, 0:n], -MASKED, MASKED,
                                                      ALU.mult, ALU.add), "put")
            masks[t] = (kp, pt, m_keep, m_put)

        def scores(t):
            k = t % TPB
            lo, hi, n, _ = window(t)
            q, ready = q_ready.pop(t)
            bank = score_bank.next()
            pe.wait(ready, [ctx_ready[t - k + i] for i in range(lo, hi + 1)], bank.free)
            keys = slice(lo * P, (hi + 1) * P)
            for c in range(KC):
                for f in products(bank.ap[:, 0:n], [q.ap[:, i, c * P:(c + 1) * P] for i in (0, 1)],
                                  (keyT_h[:, c, keys], keyT_l[:, c, keys]), n, c == 0, c == KC - 1):
                    m = pe.do(f, "scores")
            q.free = [m]
            scored[t] = (bank, m)

        def exponentials(t):
            n = window(t)[2]
            bank, m = scored.pop(t)
            kp, pt, m_keep, m_put = masks.pop(t)
            sm = soft[:, t % 8, :]
            dve.wait(m, m_keep, score.free)
            m = dve.do(lambda e: e.scalar_tensor_tensor(out=score.ap[:, 0:n], in0=bank.ap[:, 0:n], scalar=BAND_SCALE,
                                                        in1=kp.ap[:, 0:n], op0=ALU.mult, op1=ALU.mult), "kept")
            bank.free = kp.free = [m]
            dve.wait(m, m_put)
            m = dve.do(lambda e: e.tensor_tensor_reduce(score.ap[:, 0:n], score.ap[:, 0:n], pt.ap[:, 0:n], 1.0,
                                                        MASKED, ALU.add, ALU.max, sm[:, 0:1]), "score_max")
            pt.free = [m]
            dve.wait(m)
            m = dve.do(lambda e: e.tensor_scalar(sm[:, 1:2], sm[:, 0:1], -1.0, None, ALU.mult), "neg_max")
            p = prob.next()
            act.wait(m, p.free)
            m_out = act.do(lambda e: e.activation(sm[:, 2:3], masked_col[:, :], ACT.Exp, bias=sm[:, 1:2]), "masked_prob")
            m_exp = act.do(lambda e: e.activation(p.ap[:, 0:n], score.ap[:, 0:n], ACT.Exp, bias=sm[:, 1:2],
                                                  accum_out=sm[:, 3:4]), "prob")
            score.free = [m_exp]
            probs[t] = (p, [m_out, m_exp])

        def turn_probabilities(t):
            n = window(t)[2]
            p, ready = probs.pop(t)
            sm = soft[:, t % 8, :]
            dve.wait(ready)
            m_less = dve.do(lambda e: e.tensor_scalar(p.ap[:, 0:n], p.ap[:, 0:n], sm[:, 2:3], None, ALU.subtract),
                            "prob_less")
            m = dve.do(lambda e: e.scalar_tensor_tensor(out=sm[:, 4:5], in0=sm[:, 2:3], scalar=float(SEQ - n),
                                                        in1=sm[:, 3:4], op0=ALU.mult, op1=ALU.add), "band_den")
            dve.wait(m)
            m_r = dve.do(lambda e: e.reciprocal(sm[:, 5:6], sm[:, 4:5]), "band_rden")
            pe.wait(m_less)
            turned = transposes(probT_bank, [p.ap[:, i * P:(i + 1) * P] for i in range(n // P)], "probT")
            p.free = [turned]
            view = Slot(probT_bank.ap[:, 0:n])
            pt = probT.next()
            ready = split_bank(view, turned, pt.ap[:, 0, 0:n], pt.ap[:, 1, 0:n], pt.free, "probT")
            probT_bank.free = view.free
            probTs[t] = (pt, ready, m_r)

        def mix(t):
            lo, _, n, _ = window(t)
            pt, ready, m_r = probTs.pop(t)
            bank = out_bank.next()
            pe.wait(ready, bank.free)
            for i in range(n // P):
                for f in products(bank.ap[:, :], [pt.ap[:, h, i * P:(i + 1) * P] for h in (0, 1)],
                                  (ctx_h[:, lo + i, :], ctx_l[:, lo + i, :]), DIM, i == 0, i == n // P - 1):
                    m = pe.do(f, "mix")
            pt.free = [m]
            read_by[t] = m
            mixes[t] = (bank, m, m_r)

        def add_x(t):
            bank, m, m_r = mixes.pop(t)
            sm = soft[:, t % 8, :]
            tot, m_tot = totals[t // TPB]
            dve.wait(m, m_tot, mixed.free)
            m = dve.do(lambda e: e.scalar_tensor_tensor(out=mixed.ap[:, :], in0=tot.ap[:, :], scalar=sm[:, 2:3],
                                                        in1=bank.ap[:, :], op0=ALU.mult, op1=ALU.add), "mixed")
            bank.free = [m]
            tot.free = [m]
            slot, _ = x_tile[t]
            x1 = x1_out.next()
            dve.wait(m, m_r, x1.free)
            m = dve.do(lambda e: e.scalar_tensor_tensor(out=x1.ap[:, :], in0=mixed.ap[:, :], scalar=sm[:, 5:6],
                                                        in1=slot.ap[:, :], op0=ALU.mult, op1=ALU.add), "x1")
            mixed.free = [m]
            slot.free = [m]
            b, r = rows(t)
            sp.wait(m)
            x1_stored[t] = sp.do(lambda e: e.dma_start(x1_dram[b, r:r + P, :], x1.ap[:, :]), f"x1_store{t % 2}", 16)
            x1_tile[t] = (x1, statistics(x1.ap[:, :], m, moments[:, 4 + t % 4, :]))

        def put_stream(t):
            x1, ready = x1_tile.pop(t)
            so = s_out.next()
            m = normalise(x1.ap[:, :], so.ap[:, :], moments[:, 4 + t % 4, :], [ready, so.free])
            b, r = rows(t)
            sp.wait(m)
            stream_stored[0][t] = sp.do(lambda e: e.dma_start(stream[0][b, 1 + r:1 + r + P, :], so.ap[:, :]),
                                        f"s_store{t % 2}", 16)
            x1.free = [x1_stored[t], m]
            so.free = [stream_stored[0][t]]

        stages = [(mix, 5), (turn_probabilities, 4), (scores, 3), (query_statistics, 1), (make_masks, 2),
                  (exponentials, 3), (add_x, 5), (turn_query, 2), (prepare_ctx, 1), (put_stream, 6),
                  (normalise_query, 1)]
        weights = []
        summed = 0
        for s in range(TILES + 7):
            if s < TILES:
                load(s)
            while summed < min(s + 4, TILES):
                add_to_sum(summed)
                summed += 1
            for stage, after in stages:
                if 0 <= s - after < TILES:
                    stage(s - after)
            if s == 3:
                weights = load_attend_weights(0, None)
        return weights

    def attend_phase(l, src, dst, load_weights, start_after):
        plan = Plan(attend_weights_end)
        sfx = f"_{l}"
        kT = plan.tensor("kT" + sfx, [P, HEADS, SEQ], F32R)
        v_rows = plan.tensor("v_rows" + sfx, [P, TPB, HEADS * HD])
        h_in = Ring([Slot(plan.tensor(f"s_in{i}" + sfx, [P, DIM])) for i in range(3)])
        res_in = Ring([Slot(plan.tensor(f"s_res{i}" + sfx, [P, DIM])) for i in range(2)])
        hT = Ring([Slot(plan.tensor(f"hT{i}" + sfx, [P, 2, DIM], F32R)) for i in range(2)])
        square = Slot(plan.tensor("square" + sfx, [P, 2, DIM]))
        with_cos = Slot(plan.tensor("with_cos" + sfx, [P, 2, DIM]))
        with_sin = Slot(plan.tensor("with_sin" + sfx, [P, 2, DIM]))
        turned_qk = Slot(plan.tensor("turned_qk" + sfx, [P, 2, DIM]))
        qT = Ring([Slot(plan.tensor(f"qT{i}" + sfx, [P, HEADS, 2, P], F32R)) for i in range(2)])
        rope_cos = plan.tensor("rope_cos" + sfx, [P, TPB, 2 * HD])
        rope_sin = plan.tensor("rope_sin" + sfx, [P, TPB, 2 * HD])
        scales = plan.tensor("scales" + sfx, [P, 2 * HD])
        far = plan.tensor("far" + sfx, [P, WIN])
        score = Ring([Slot(plan.tensor(f"lscore{i}" + sfx, [P, WIN])) for i in range(3)])
        prob = Ring([Slot(plan.tensor(f"lprob{i}" + sfx, [P, WIN])) for i in range(3)])
        probT = Ring([Slot(plan.tensor(f"lprobT{i}" + sfx, [P, WIN])) for i in range(3)])
        o_rows = Slot(plan.tensor("o_rows" + sfx, [P, DIM]))
        oT = Slot(plan.tensor("oT" + sfx, [P, 2, DIM], F32R))
        s_out = Ring([Slot(plan.tensor(f"a_out{i}" + sfx, [P, DIM])) for i in range(2)])

        qk_banks = Slot(bank_pair)
        vy_bank = Slot(banks[0])
        turn_banks = Ring([Slot(banks[1]), Slot(banks[2])])
        score_banks = Ring([Slot(banks[3]), Slot(banks[4])])
        o_bank = Slot(banks[5])
        for q in (sp, pe, act, dve, pool):
            q.wait(start_after)

        m = [sp.do(lambda e: e.dma_start(rope_cos[:, :, :], consts["rope_cos"]), "rope_in", 16),
             sp.do(lambda e: e.dma_start(rope_sin[:, :, :], consts["rope_sin"]), "rope_in", 16),
             sp.do(lambda e: e.dma_start(scales[:, 0:HD], q_scale[l].partition_broadcast(P)), "rope_in", 16),
             sp.do(lambda e: e.dma_start(scales[:, HD:], k_scale[l].partition_broadcast(P)), "rope_in", 16),
             sp.do(lambda e: e.dma_start(far[:, :], consts["far"]), "rope_in", 16)]
        pool.wait(m[-1])
        spread = scales[:, :].unsqueeze(1).to_broadcast([P, TPB, 2 * HD])
        m_cos = pool.do(lambda e: e.tensor_tensor(rope_cos[:, :, :], rope_cos[:, :, :], spread, ALU.mult), "rope_scaled")
        m_sin = pool.do(lambda e: e.tensor_tensor(rope_sin[:, :, :], rope_sin[:, :, :], spread, ALU.mult), "rope_scaled")
        rope_ready, far_ready = [m_cos, m_sin], m[-1]
        m_zero = []
        for s in qT.slots:
            pool.wait(m_sin, m_zero)
            m_zero.append(pool.do(lambda e, s=s: e.memset(s.ap[HD:, :, 1, :].bitcast(F32), 0.0), "qT_zero"))
        pool.wait(m_zero)

        h_tile, res_tile, h_slot, v_ready, qk_ready, q_slot, k_ready = ({} for _ in range(7))
        attended, done = [None] * TILES, {}

        def load(t):
            b, r = rows(t)
            slot = h_in.next()
            sp.wait(slot.free, stream_stored[src][t], zero_rows[-1], stream_stored[src][t - 1] if t else None)
            sp.do(lambda e: e.dma_start(slot.ap[:, 0:HALF], stream[src][b, 1 + r:1 + r + P, 0:HALF]), f"s_in{t % 3}", 16)
            h_tile[t] = (slot, sp.do(lambda e: e.dma_start(slot.ap[:, HALF:], stream[src][b, r:r + P, HALF:]),
                                     f"s_in{t % 3}", 16))

        def load_res(t):
            b, r = rows(t)
            slot = res_in.next()
            sp.wait(slot.free)
            res_tile[t] = (slot, sp.do(lambda e: e.dma_start(slot.ap[:, :], stream[src][b, 1 + r:1 + r + P, :]),
                                       f"s_res{t % 2}", 16))

        def turn_h(t):
            slot, loaded = h_tile[t]
            pe.wait(loaded)
            bank = turn_banks.next()
            turned = transposes(bank, [slot.ap[:, c * P:(c + 1) * P] for c in range(KC)], "h_turned")
            slot.free = [turned]
            h = hT.next()
            ready = split_bank(bank, turned, h.ap[:, 0, :], h.ap[:, 1, :], h.free, "hT")
            h_slot[t] = (h, ready)

        def project_pieces(t):
            h, ready = h_slot[t]
            pieces = []
            for part, bank in ((2, vy_bank.ap[:, :]), (0, qk_banks.ap[:, 0, :]), (1, qk_banks.ap[:, 1, :])):
                for c in range(KC):
                    cols = slice(part * DIM, (part + 1) * DIM)
                    fs = products(bank, [h.ap[:, i, c * P:(c + 1) * P] for i in (0, 1)],
                                  (wqkv_h[:, c, cols], wqkv_l[:, c, cols]), DIM, c == 0, c == KC - 1)
                    pieces += [(part, c, i, f) for i, f in enumerate(fs)]
            marks = {}

            def emit(piece):
                part, c, i, f = piece
                if (c, i) == (0, 0):
                    pe.wait(ready, weights_ready, vy_bank.free if part == 2 else qk_banks.free)
                last = (c, i) == (KC - 1, 2)
                m = pe.do(f, "projected" if last else None)
                if last:
                    marks[part] = m
                    if part == 2:
                        old = attended[t - TPB + 2] if t >= TPB else None
                        act.wait(m, old)
                        v_ready[t] = act.do(lambda e: e.activation(v_rows[:, t % TPB, :], vy_bank.ap[:, :], ACT.Copy),
                                            "v_rows")
                        vy_bank.free = [v_ready[t]]
                    if part == 1:
                        h.free = [m]
                        qk_ready[t] = [marks[0], m]
            return [lambda p=p: emit(p) for p in pieces]

        def rope_steps(t):
            k = t % TPB
            nm = norm[:, t % 2, :]
            act.wait(qk_ready[t], square.free)
            flat = lambda s: s[:, :, :].rearrange("p a n -> p (a n)")
            m_sq = act.do(lambda e: e.activation(flat(square.ap), flat(qk_banks.ap), ACT.Square), "squared")
            table = lambda s: s[:, k, :].rearrange("p (a d) -> p a d", a=2).unsqueeze(2).to_broadcast([P, 2, HEADS, HD])
            by_head = lambda s: s[:, :, :].rearrange("p a (h d) -> p a h d", h=HEADS)
            heads16 = lambda s: s[:, :, :].rearrange("p a (h d) -> p (a h) d", d=HD)
            marks = {}

            def reduce():
                dve.wait(m_sq)
                m = dve.do(lambda e: e.tensor_reduce(nm[:, 0:16], heads16(square.ap), AX, ALU.add), "norm_sum")
                square.free = [m]
                pool.wait(m)
                m = pool.do(lambda e: e.tensor_scalar(nm[:, 0:16], nm[:, 0:16], NORM_FLOOR ** 2, 0.0, ALU.max, ALU.add),
                            "norm_floor")
                pool.wait(m)
                marks["r"] = pool.do(lambda e: e.tensor_tensor(nm[:, 16:32], nm[:, 0:16], half_power[:, :], ALU.pow),
                                     "norm_inverse")

            def cos():
                dve.wait(qk_ready[t], rope_ready, with_cos.free, m_sq)
                marks["cos"] = dve.do(lambda e: e.tensor_tensor(by_head(with_cos.ap), by_head(qk_banks.ap),
                                                                table(rope_cos), ALU.mult), "with_cos")

            def sin():
                dve.wait(with_sin.free)
                marks["sin"] = dve.do(lambda e: e.tensor_tensor(by_head(with_sin.ap), by_head(qk_banks.ap),
                                                                table(rope_sin), ALU.mult), "with_sin")
                qk_banks.free = [marks["sin"]]

            def combine():
                pool.wait(marks["cos"], marks["sin"], turned_qk.free)
                h2 = HD // 2
                for a, b in ((0, h2), (h2, 0)):
                    m = pool.do(lambda e, a=a, b=b: e.tensor_tensor(
                        heads16(turned_qk.ap)[:, :, a:a + h2], heads16(with_cos.ap)[:, :, a:a + h2],
                        heads16(with_sin.ap)[:, :, b:b + h2], ALU.add), "rotated")
                with_cos.free = with_sin.free = [m]
                pool.wait(m, marks["r"])
                inv = nm[:, 16:32].unsqueeze(2).to_broadcast([P, 16, HD])
                marks["qk"] = pool.do(lambda e: e.tensor_tensor(heads16(turned_qk.ap), heads16(turned_qk.ap), inv,
                                                                ALU.mult), "qk_scaled")
            return [reduce, cos, sin, combine], marks

        lo, hi = slice(0, HD), slice(HD, P)

        def pairs(bank, half):
            return bank.ap[half, :].rearrange("p (i n) -> p i n", i=4)

        def turn_q(t, scaled):
            pe.wait(scaled)
            bank, q = turn_banks.next(), qT.next()
            turned = transposes(bank, [turned_qk.ap[:, 0, i * P:(i + 1) * P] for i in range(4)], "q_turned")
            marks = []
            act.wait(turned, q.free)
            dve.wait(turned, q.free)
            for odd, here in ((0, lo), (1, hi)):
                source = pairs(bank, here)
                for where in (here, hi if here is lo else lo):
                    marks.append(act.do(lambda e, source=source, where=where, odd=odd: e.activation(
                        q.ap[where, odd::2, 0, :], source, ACT.Copy), "qT_high"))
                dve.wait(marks[-1])
                marks.append(dve.do(lambda e, source=source, here=here, odd=odd: e.tensor_tensor(
                    q.ap[lo, odd::2, 1, :], source, q.ap[here, odd::2, 0, :].bitcast(F32), ALU.subtract), "qT_low"))
            bank.free = [marks[-1]]
            q_slot[t] = (q, marks + m_zero)

        def turn_k(t):
            k = t % TPB
            bank = turn_banks.next()
            turned = transposes(bank, [turned_qk.ap[:, 1, i * P:(i + 1) * P] for i in range(4)], "k_turned")
            turned_qk.free = [turned]
            old = attended[t - TPB + 2] if t >= TPB else None
            act.wait(turned, old)
            dve.wait(turned, old)
            cols = slice(k * P, (k + 1) * P)
            marks = []
            for odd, here in ((0, lo), (1, hi)):
                source = pairs(bank, here)
                m = act.do(lambda e, source=source, odd=odd: e.activation(kT[lo, odd::2, cols], source, ACT.Copy),
                           "kT_high")
                dve.wait(m)
                marks += [m, dve.do(lambda e, source=source, odd=odd: e.tensor_tensor(
                    kT[hi, odd::2, cols], source, kT[lo, odd::2, cols].bitcast(F32), ALU.subtract), "kT_low")]
            bank.free = [marks[-1]]
            k_ready[t] = marks

        def normalise_out(t):
            m_den, m_mix = done[t]
            sm = small[:, t % 2, :]
            dve.wait(m_den)
            m = dve.do(lambda e: e.reciprocal(sm[:, 16:24], sm[:, 8:16]), "lrden")
            dve.wait(m, m_mix, o_rows.free)
            m = dve.do(lambda e: e.tensor_tensor(
                o_rows.ap[:, :].rearrange("p (h d) -> p h d", h=HEADS),
                o_bank.ap[:, :].rearrange("p (h d) -> p h d", h=HEADS),
                sm[:, 16:24].unsqueeze(2).to_broadcast([P, HEADS, HD]), ALU.mult), "o_rows")
            o_bank.free = [m]
            done[t] = m

        def turn_out(t):
            pe.wait(done[t])
            bank = turn_banks.next()
            turned = transposes(bank, [o_rows.ap[:, c * P:(c + 1) * P] for c in range(KC)], "o_turned")
            o_rows.free = [turned]
            done[t] = split_bank(bank, turned, oT.ap[:, 0, :], oT.ap[:, 1, :], oT.free, "oT")

        def project_out(t, half):
            if half == 0:
                pe.wait(done[t], weights_ready, vy_bank.free)
            for c in (0, 1) if half == 0 else (2, 3):
                for f in products(vy_bank.ap[:, :], [oT.ap[:, i, c * P:(c + 1) * P] for i in (0, 1)],
                                  (wo_h[:, c, :], wo_l[:, c, :]), DIM, c == 0, c == KC - 1):
                    m = pe.do(f, "wo_done")
            if half == 1:
                oT.free = [m]
                done[t] = m

        def add_residual(t):
            slot, loaded = res_tile[t]
            so = s_out.next()
            dve.wait(done[t], loaded, so.free)
            m = dve.do(lambda e: e.tensor_tensor(so.ap[:, :], vy_bank.ap[:, :], slot.ap[:, :], ALU.add), "a_out")
            vy_bank.free = [m]
            slot.free = [m]
            b, r = rows(t)
            sp.wait(m)
            stream_stored[dst][t] = sp.do(lambda e: e.dma_start(stream[dst][b, 1 + r:1 + r + P, :], so.ap[:, :]),
                                          f"a_store{t % 2}", 16)
            so.free = [stream_stored[dst][t]]

        def step(s):
            t, tail = s - 2, s - 3
            live = 0 <= t < TILES
            ended = 0 <= tail < TILES
            pieces = project_pieces(s) if s < TILES else []
            fillers, marks = rope_steps(s - 1) if 1 <= s <= TILES else ([], None)
            if live:
                k = t % TPB
                w = min(k, 2) + 1
                n = w * P
                first = (k - w + 1) * P
                q, q_marks = q_slot[t]
                sm = small[:, t % 2, :]
                keys_ready = [k_ready[t - i] for i in range(w)]
                load_res(t)
            if s + 3 < TILES:
                load(s + 3)
            soft = {}
            slots = HEADS + 2
            for i in range(slots):
                if ended and i == 0:
                    normalise_out(tail)
                if live and i < HEADS:
                    bank, sc, p = score_banks.next(), score.next(), prob.next()
                    pe.wait(q_marks, keys_ready, bank.free)
                    for part in (0, 1):
                        m = pe.do(lambda e, part=part, i=i, bank=bank: e.matmul(
                            bank.ap[:, 0:n], q.ap[:, i, part, :], kT[:, i, first:first + n],
                            start=(part == 0), stop=(part == 1)), "lscores" if part else None)
                    if i == HEADS - 1:
                        q.free = [m]
                    dve.wait(m, sc.free, far_ready)
                    m = dve.do(lambda e, i=i, bank=bank, sc=sc: e.tensor_tensor_reduce(
                        sc.ap[:, 0:n], bank.ap[:, 0:n], far[:, WIN - n:], 1.0, BIG, ALU.add, ALU.min,
                        sm[:, i:i + 1]), "lmax")
                    bank.free = [m]
                    act.wait(m, p.free)
                    m = act.do(lambda e, i=i, sc=sc, p=p: e.activation(
                        p.ap[:, 0:n], sc.ap[:, 0:n], ACT.Exp, bias=sm[:, i:i + 1], scale=-1.0,
                        accum_out=sm[:, 8 + i:9 + i]), "lprob")
                    sc.free = [m]
                    soft[i] = (p, m)
                    m_den = m
                if i < len(fillers):
                    fillers[i]()
                for f in pieces[len(pieces) * i // slots: len(pieces) * (i + 1) // slots]:
                    f()
                if ended and i == 1:
                    turn_out(tail)
                if live and 1 <= i <= HEADS:
                    p, m = soft[i - 1]
                    pe.wait(m)
                    bank, pt = turn_banks.next(), probT.next()
                    turned = transposes(bank, [p.ap[:, j * P:(j + 1) * P] for j in range(w)], "lprobT")
                    p.free = [turned]
                    eng = act if i % 2 else dve
                    eng.wait(turned, pt.free)
                    if eng is act:
                        m = act.do(lambda e, bank=bank, pt=pt: e.activation(pt.ap[:, 0:n], bank.ap[:, 0:n], ACT.Copy),
                                   "lprobT_a")
                    else:
                        m = dve.do(lambda e, bank=bank, pt=pt: e.tensor_copy(pt.ap[:, 0:n], bank.ap[:, 0:n]),
                                   "lprobT_v")
                    bank.free = [m]
                    soft[i - 1] = (pt, m)
                if live and i >= 2:
                    h = i - 2
                    pt, m = soft[h]
                    pe.wait(m, [v_ready[t - j] for j in range(w)], o_bank.free)
                    for j in range(w):
                        m = pe.do(lambda e, j=j, h=h, pt=pt: e.matmul(
                            o_bank.ap[:, h * HD:(h + 1) * HD], pt.ap[:, j * P:(j + 1) * P],
                            v_rows[:, k - w + 1 + j, h * HD:(h + 1) * HD], start=(h == 0 and j == 0),
                            stop=(j == w - 1), skip_group_check=True), "lmix" if j == w - 1 else None)
                    pt.free = [m]
                if i == 4 and s + 1 < TILES:
                    turn_h(s + 1)
                if ended and i in (5, 6):
                    project_out(tail, i - 5)
                if ended and i == 7:
                    add_residual(tail)
                if marks and i == 7:
                    turn_q(s - 1, marks["qk"])
                if marks and i == 8:
                    turn_k(s - 1)
            if live:
                attended[t] = m
                done[t] = (m_den, m)

        for t in range(3):
            load(t)
        weights_ready = load_weights()
        turn_h(0)
        for s in range(TILES + 3):
            step(s)

    def ffn_phase(l, src, dst, start_after):
        plan = Plan(phase_base)
        sfx = f"_f{l}"
        w1_h, w1_raw = plan.pair("w1_h" + sfx, [P, KC, 2 * HID])
        w1_l = plan.tensor("w1_l" + sfx, [P, KC, 2 * HID], F32R)
        w2_h, w2_raw = plan.pair("w2_h" + sfx, [P, HC, DIM])
        w2_l = plan.tensor("w2_l" + sfx, [P, HC, DIM], F32R)
        hT = Ring([Slot(plan.tensor(f"fhT{i}" + sfx, [P, 2, KC, GROUP * P], F32R)) for i in range(2)])
        uT = Ring([Slot(plan.tensor(f"uT{i}" + sfx, [P, 2, GROUP * P], F32R)) for i in range(3)])
        gate = Ring([Slot(plan.tensor(f"gate{i}" + sfx, [P, GROUP * P])) for i in range(2)])
        u = Ring([Slot(plan.tensor(f"u{i}" + sfx, [P, GROUP * P])) for i in range(2)])
        gain = plan.tensor("gain" + sfx, [P, DIM])
        shift = plan.tensor("shift" + sfx, [P, DIM])
        bias2 = plan.tensor("bias2" + sfx, [P, DIM])
        bias1 = plan.tensor("bias1" + sfx, [P, 2, HC])
        h_in = Ring([Slot(plan.tensor(f"h_in{i}" + sfx, [P, DIM])) for i in range(2)])
        h_norm = Ring([Slot(plan.tensor(f"h_norm{i}" + sfx, [P, DIM])) for i in range(2)])
        res = Ring([Slot(plan.tensor(f"res{i}" + sfx, [P, DIM])) for i in range(3)])
        add_x1 = l == DEPTH - 1
        x1_in = Ring([Slot(plan.tensor(f"x1_in{i}" + sfx, [P, DIM])) for i in range(1)]) if add_x1 else None

        y_banks = [Slot(bank_pair[:, 0, :]), Slot(bank_pair[:, 1, :]), Slot(banks[0][:, :]), Slot(banks[1][:, :])]
        h_banks = Ring([Slot(banks[2]), Slot(banks[3]), Slot(banks[4])])
        turn_bank = Slot(banks[5])
        for q in (sp, pe, act, dve, pool):
            q.wait(start_after)

        for i, (dst_ap, src_ap) in enumerate(((gain[:, :], ln_g[l].partition_broadcast(P)),
                                              (shift[:, :], ln_b[l].partition_broadcast(P)),
                                              (bias2[:, :], b2[l].partition_broadcast(P)))):
            sp.do(lambda e, d=dst_ap, s=src_ap: e.dma_start(d, s), "ffn_vectors", 16)
        full = HC - 1
        for half in (0, 1):
            v = b1[l, half * HID:(half + 1) * HID]
            sp.do(lambda e, v=v, half=half: e.dma_start(bias1[:, half, 0:full],
                                                        v[0:full * P].rearrange("(j p) -> p j", p=P)), "ffn_vectors", 16)
            vectors = sp.do(lambda e, v=v, half=half: e.dma_start(bias1[0:hid_rows(full), half, full:HC],
                                                                  v[full * P:HID].unsqueeze(1)), "ffn_vectors", 16)
        w1v = w1[l].rearrange("(c p) n -> p c n", p=P)
        w1_ready, w2_ready = {}, {}
        chunks = [(0, 1), (1, 2), (2, 4), (4, 7), (7, HC)]

        def load_weights(i):
            a, b = chunks[i]
            pieces = []
            for half in (0, 1):
                cols = slice(half * HID + a * P, half * HID + min(b * P, HID))
                loaded = sp.do(lambda e, cols=cols: e.dma_start(w1_raw[:, :, cols], w1v[:, :, cols]), f"w1_in{i}", 16)
                pieces.append((cols, loaded))
            for cols, _ in pieces:
                m = split_weight(dve, w1_h[:, :, cols], w1_l[:, :, cols], w1_raw[:, :, cols], loaded, "weight")
            for j in range(a, b):
                w1_ready[j] = m
            whole = min(b, full)
            if whole > a:
                loaded = sp.do(lambda e: e.dma_start(w2_raw[:, a:whole, :], w2[l, a * P:whole * P].rearrange(
                    "(j p) n -> p j n", p=P)), f"w2_in{i}", 16)
                m = split_weight(dve, w2_h[:, a:whole, :], w2_l[:, a:whole, :], w2_raw[:, a:whole, :], loaded, "weight")
                for j in range(a, whole):
                    w2_ready[j] = m
            if b == HC:
                r = hid_rows(full)
                loaded = sp.do(lambda e: e.dma_start(w2_raw[0:r, full, :], w2[l, full * P:HID]), "w2_tail_in", 16)
                w2_ready[full] = split_weight(dve, w2_h[0:r, full, :], w2_l[0:r, full, :], w2_raw[0:r, full, :],
                                              loaded, "weight")

        h_slots, h_marks = {}, {}

        tiles = {}

        def load(t):
            b, r = rows(t)
            slot = h_in.next()
            sp.wait(slot.free, stream_stored[src][t], zero_rows[-1], stream_stored[src][t - 1] if t else None)
            sp.do(lambda e: e.dma_start(slot.ap[:, 0:HALF], stream[src][b, 1 + r:1 + r + P, 0:HALF]), f"h_in{t % 2}", 16)
            loaded = sp.do(lambda e: e.dma_start(slot.ap[:, HALF:], stream[src][b, r:r + P, HALF:]), f"h_in{t % 2}", 16)
            tiles[t] = (slot, loaded)

        def normalise(t):
            slot, loaded = tiles[t]
            hn = h_norm.next()
            dve.wait(hn.free)
            m = layer_norm(slot.ap[:, :], [slot.ap[:, :]], hn.ap[:, :], loaded, t % 2, "ln")
            slot.free = [m]
            pool.wait(m, vectors)
            m = pool.do(lambda e: e.tensor_tensor(hn.ap[:, :], hn.ap[:, :], gain[:, :], ALU.mult), "gained")
            pool.wait(m)
            m = pool.do(lambda e: e.tensor_tensor(hn.ap[:, :], hn.ap[:, :], shift[:, :], ALU.add), "shifted")
            tiles[t] = (hn, m)

        def turn(t):
            g, i = divmod(t, GROUP)
            hn, m = tiles.pop(t)
            pe.wait(m)
            turned = transposes(turn_bank, [hn.ap[:, c * P:(c + 1) * P] for c in range(KC)], "fh_turned")
            hn.free = [turned]
            if i == 0:
                h_slots[g], h_marks[g] = hT.next(), []
            h = h_slots[g]
            view = Slot(turn_bank.ap[:, :].rearrange("p (c n) -> p c n", c=KC))
            h_marks[g] += split_bank(view, turned, h.ap[:, 0, :, i * P:(i + 1) * P], h.ap[:, 1, :, i * P:(i + 1) * P],
                                     h.free, "fhT")
            turn_bank.free = view.free

        def up(g, j):
            n = hid_rows(j)
            h = h_slots[g]
            marks, bank_of = {}, {}
            for half in (1, 0):
                bank = h_banks.next()
                bank_of[half] = bank
                cols = slice(half * HID + j * P, half * HID + j * P + n)
                pe.wait(h_marks[g], w1_ready[j], bank.free)
                for c in range(KC):
                    fs = [lambda e, a=a, b=b, s=s, p=p, bank=bank: e.matmul(bank.ap[0:n, :], a, b, start=s, stop=p)
                          for a, b, s, p in ((w1_h[:, c, cols], h.ap[:, 0, c, :], c == 0, False),
                                             (w1_h[:, c, cols], h.ap[:, 1, c, :], False, False),
                                             (w1_l[:, c, cols], h.ap[:, 0, c, :], False, c == KC - 1))]
                    for f in fs:
                        m = pe.do(f, "up")
                marks[half] = m
            if j == HC - 1:
                h.free = [m]
            gt, uu, ut = gate.next(), u.next(), uT.next()
            act.wait(marks[1], gt.free, vectors)
            m = act.do(lambda e: e.activation(gt.ap[0:n, :], bank_of[1].ap[0:n, :], ACT.Gelu,
                                              bias=bias1[0:n, 1, j:j + 1]), "gate")
            bank_of[1].free = [m]
            dve.wait(m, marks[0], uu.free, vectors)
            m = dve.do(lambda e: e.scalar_tensor_tensor(out=uu.ap[0:n, :], in0=bank_of[0].ap[0:n, :],
                                                        scalar=bias1[0:n, 0, j:j + 1], in1=gt.ap[0:n, :],
                                                        op0=ALU.add, op1=ALU.mult), "u")
            bank_of[0].free = gt.free = [m]
            act.wait(m, ut.free)
            m_h = act.do(lambda e: e.activation(ut.ap[0:n, 0, :], uu.ap[0:n, :], ACT.Copy), "uT_high")
            dve.wait(m_h, ut.free)
            m_l = dve.do(lambda e: e.tensor_tensor(ut.ap[0:n, 1, :], uu.ap[0:n, :], ut.ap[0:n, 0, :].bitcast(F32),
                                                   ALU.subtract), "uT_low")
            uu.free = [m_l]
            return ut, [m_h, m_l]

        def down(j, ut, ready):
            n = hid_rows(j)
            pe.wait(ready, w2_ready[j])
            marks = []
            for i in range(GROUP):
                if j == 0:
                    pe.wait(y_banks[i].free)
                for f in products(y_banks[i].ap, [ut.ap[0:n, h, i * P:(i + 1) * P] for h in (0, 1)],
                                  (w2_h[0:n, j, :], w2_l[0:n, j, :]), DIM, j == 0, j == HC - 1):
                    m = pe.do(f, "down")
                marks.append(m)
            ut.free = [m]
            return marks

        residual = {}

        def load_residual(t):
            b, r = rows(t)
            slot = res.next()
            sp.wait(slot.free)
            loaded = sp.do(lambda e: e.dma_start(slot.ap[:, :], stream[src][b, 1 + r:1 + r + P, :]), f"res_in{t % 3}", 16)
            pool.wait(loaded, vectors)
            m = pool.do(lambda e: e.tensor_tensor(slot.ap[:, :], slot.ap[:, :], bias2[:, :], ALU.add), "res_bias")
            if add_x1:
                xs = x1_in.next()
                sp.wait(xs.free, x1_stored[t])
                loaded = sp.do(lambda e: e.dma_start(xs.ap[:, :], x1_dram[b, r:r + P, :]), "x1_in", 16)
                pool.wait(loaded, m)
                m = pool.do(lambda e: e.tensor_tensor(slot.ap[:, :], slot.ap[:, :], xs.ap[:, :], ALU.add), "res_x1")
                xs.free = [m]
            residual[t] = (slot, m)

        def finish(t, m_y):
            b, r = rows(t)
            i = t % GROUP
            slot, m = residual.pop(t)
            dve.wait(m, m_y)
            m = dve.do(lambda e: e.tensor_tensor(slot.ap[:, :], y_banks[i].ap, slot.ap[:, :], ALU.add), "f_out")
            y_banks[i].free = [m]
            sp.wait(m)
            target = out[b, r:r + P, :] if add_x1 else stream[dst][b, 1 + r:1 + r + P, :]
            m = sp.do(lambda e: e.dma_start(target, slot.ap[:, :]), f"f_store{t % 3}", 16)
            slot.free = [m]
            if not add_x1:
                stream_stored[dst][t] = m

        def finish_group(g, marks):
            for i in range(GROUP):
                if i == GROUP - 1:
                    load_residual(g * GROUP + i)
                finish(g * GROUP + i, marks[i])

        load(0)
        load(1)
        load_weights(0)
        for t in range(GROUP):
            normalise(t)
            if t + 2 < GROUP:
                load(t + 2)
            turn(t)
        pending = None
        for g in range(GROUPS):
            for j in range(HC):
                ut, ready = up(g, j)
                if g == 0 and j + 1 < len(chunks):
                    load_weights(j + 1)
                if pending:
                    marks = down(*pending)
                    if j == 0:
                        finish_group(g - 1, marks)
                pending = (j, ut, ready)
                i, later = divmod(j, 2)
                following = (g + 1) * GROUP + i
                if g + 1 < GROUPS:
                    if later == 0 and i < GROUP:
                        load(following)
                    if later == 1 and i < GROUP:
                        normalise(following)
                    if later == 1 and 1 <= i <= GROUP:
                        turn(following - 1)
                if later == 0 and 2 <= i < 5:
                    load_residual(g * GROUP + i - 2)
        finish_group(GROUPS - 1, down(*pending))

    def everything():
        return [(s, s.value) for s in signals.values()]

    first_weights = band_phase()
    for l in range(DEPTH):
        after = everything()
        attend_phase(l, 2 * l, 2 * l + 1, (lambda: load_attend_weights(l, after)) if l else (lambda: first_weights), after)
        ffn_phase(l, 2 * l + 1, 2 * l + 2, everything())
    sp.wait(everything())

    with nc.allow_non_contiguous_dma(reason="bias columns"), nc.Block() as block:
        block.sync(sp.run)
        block.tensor(pe.run)
        block.scalar(act.run)
        block.vector(dve.run)
        block.gpsimd(pool.run)


def shape_constants():
    f = np.float32
    i, j = np.arange(P)[:, None], np.arange(WIN)[None, :]
    band01 = (np.abs(i - (j - P)) <= P).astype(f)
    back = i - (j - 2 * P)
    far = np.where((back < 0) | (back > 2 * P), f(BIG), f(0)).astype(f)
    half_idx = np.arange(0, HD, 2, dtype=f)
    inv_freq = f(1.0) / f(10000.0) ** (half_idx / f(HD))
    t = np.arange(SEQ, dtype=f)
    freqs = t[:, None] * inv_freq[None, :]
    base = (half_idx + f(0.4 * HD)) / f(1.4 * HD)
    power = (t - f(SEQ // 2)) / f(128.0)
    scale = base[None, :] ** power[:, None]
    cos, sin = np.cos(freqs), np.sin(freqs)
    c, s = [], []
    for sc, m in ((scale, -QK_SCALE), (f(1.0) / scale, 1.0)):
        c += [cos * sc * f(m), cos * sc * f(m)]
        s += [sin * sc * f(m), -sin * sc * f(m)]
    tile = lambda parts: np.ascontiguousarray(
        np.concatenate(parts, 1).astype(f).reshape(TPB, P, 2 * HD).transpose(1, 0, 2))
    return {"ident": np.eye(P, dtype=f), "zeros": np.zeros((BATCH, DIM), f), "band01": band01, "far": far,
            "rope_cos": tile(c), "rope_sin": tile(s)}


_INS = ["x", "ctx_1024", "mask_BxS2_bf1", "L0_ffn_wqkv", "L0_ffn_q_scale", "L0_ffn_k_scale", "L0_ffn_wo",
        "L0_ffn_ln_g", "L0_ffn_ln_b", "L0_ffn_w1", "L0_ffn_b1", "L0_ffn_w2", "L0_ffn_b2"]


def kernel(**inputs):
    import concourse.bacc as bacc
    from concourse.bass_utils import run_bass_kernel_spmd

    nc = bacc.Bacc("TRN2", target_bir_lowering=False, num_devices=1)
    arrays = {}

    def declare(name, a):
        a = np.ascontiguousarray(a)
        if a.dtype.kind == "b":
            a = a.view(np.uint8)
        arrays[name] = a
        return nc.dram_tensor(name, a.shape, mybir.dt.from_np(a.dtype), kind="ExternalInput").ap()

    args = [declare(f"in_{name}", inputs[name]) for name in _INS]
    consts = {name: declare(f"const_{name}", a) for name, a in shape_constants().items()}
    out = nc.dram_tensor("out_0", (BATCH, SEQ, DIM), F32, kind="ExternalOutput").ap()
    build(nc, *args, consts, out)
    r = run_bass_kernel_spmd(nc, [arrays], core_ids=[0])
    return r.results[0]["out_0"]
```

```python
import numpy as np
import concourse.bass as bass
from concourse import mybir
from concourse.alu_op_type import AluOpType as ALU

F32 = mybir.dt.float32
F32R = mybir.dt.float32r
U8 = mybir.dt.uint8
ACT = mybir.ActivationFunctionType
AX = mybir.AxisListType.X

P = 128
BATCH, SEQ, DIM = 4, 1024, 512
TPB = SEQ // P
TILES = BATCH * TPB
HALF = DIM // 2
KC = DIM // P
HEADS, HD = 8, 64
QKV = 3 * HEADS * HD
HID = int(DIM * 4 * 2 / 3)
DEPTH = 2
HC = (HID + P - 1) // P
GROUP = 4
GROUPS = TILES // GROUP
QK_SCALE = 8.0
EPS = 1e-5
NORM_FLOOR = 1e-12
MASKED = -1e9
BIG = 3.0e38
BAND_SCALE = float(np.float32(1.0) / np.sqrt(np.float32(DIM)))
WIN = 3 * P
FREE_BASE = 16512
SUM_AHEAD = 4
WEIGHTS_AT = 5
SBUF_END = 229344
BLOCK_BYTES = 2 * (2 * KC * P + DIM) * 4
LATE_BYTES = 87040
EARLY_BYTES = 37376
ATTEND_FIRST_BYTES = 20992
OUT_BYTES = 8192


def hid_rows(j):
    return min(P, HID - j * P)


class Signal:

    def __init__(self, sem):
        self.sem, self.value = sem, 0


class Queue:

    def __init__(self, signals):
        self.steps, self.passed, self.signals = [], {}, signals
        self.last = None

    def wait(self, *marks):
        for mark in marks:
            if mark is None:
                continue
            if isinstance(mark, (list, tuple)) and not (mark and isinstance(mark[0], Signal)):
                self.wait(*mark)
                continue
            signal, value = mark
            if self.passed.get(signal, 0) < value:
                self.passed[signal] = value
                self.steps.append(("wait", signal.sem, value))

    def do(self, build, signal=None, by=1):
        if signal is None:
            self.steps.append(("do", build, None, 0))
            return None
        s = self.signals(signal)
        s.value += by
        self.steps.append(("do", build, s.sem, by))
        self.last = (s, s.value)
        return self.last

    def run(self, engine):
        for kind, what, *rest in self.steps:
            if kind == "wait":
                engine.wait_ge(what, rest[0])
            else:
                ins = what(engine)
                if rest[0] is not None:
                    ins.then_inc(rest[0], rest[1])


class Slot:

    def __init__(self, ap, free=()):
        self.ap, self.free = ap, free


class Ring:
    def __init__(self, slots):
        self.slots, self.n = slots, 0

    def next(self):
        self.n += 1
        return self.slots[(self.n - 1) % len(self.slots)]


def build(nc, x, ctx, mask, wqkv, q_scale, k_scale, wo, ln_g, ln_b, w1, b1, w2, b2, consts, out):
    signals = {}

    def signal(name):
        if name not in signals:
            signals[name] = Signal(nc.alloc_semaphore(name))
        return signals[name]

    sp, pe, act, dve, pool = (Queue(signal) for _ in range(5))

    class Plan:

        def __init__(self, start, free=()):
            self.at, self.free = start, free

        def tensor(self, name, shape, dtype=F32):
            size = int(np.prod(shape[1:])) * (1 if dtype == U8 else 4)
            t = nc.alloc_sbuf_tensor_at(name, shape, dtype, offset=self.at)
            self.at += (size + 31) // 32 * 32
            return t

        def slot(self, name, shape, dtype=F32):
            return Slot(self.tensor(name, shape, dtype)[tuple(slice(None) for _ in shape)], self.free)

        def pair(self, name, shape):
            at = self.at
            t = self.tensor(name, shape, F32R)
            raw = nc.alloc_sbuf_tensor_at(name + "_raw", shape, F32, offset=at)
            return t, raw

    fixed = Plan(FREE_BASE)
    ident = fixed.tensor("ident", [P, P])
    half_power = fixed.tensor("half_power", [P, 16])
    masked_col = fixed.tensor("masked_col", [P, 1])
    stats = fixed.tensor("stats", [P, 2, 32])
    small = fixed.tensor("small", [P, 4, 32])
    norm = fixed.tensor("norm", [P, 2, 32])
    phase_base = fixed.at

    bank_pair = nc.alloc_psum_tensor("bank_pair", [P, 2, 512], F32)[:, :, :]
    banks = [nc.alloc_psum_tensor(f"bank{i}", [P, 512], F32)[:, :] for i in range(6)]

    x1_dram = nc.dram_tensor("x1_dram", [BATCH, SEQ, DIM], F32).ap()
    stream = [nc.dram_tensor(f"stream{i}", [BATCH, SEQ + 1, DIM], F32).ap() for i in range(2 * DEPTH)]
    zero_rows = [sp.do(lambda e, s=s: e.dma_start(s[:, 0, :], consts["zeros"]), "zero_rows", 16)
                 for s in stream]
    x1_stored = [None] * TILES
    stream_stored = [[None] * TILES for _ in stream]

    def rows(t):
        return t // TPB, (t % TPB) * P

    m_ident = sp.do(lambda e: e.dma_start(ident[:, :], consts["ident"]), "ident_in", 16)
    m_half = pool.do(lambda e: e.memset(half_power[:, :], -0.5), "half_power")
    m_masked = pool.do(lambda e: e.memset(masked_col[:, :], MASKED), "masked_col")
    pool.wait(m_half)
    act.wait(m_masked)
    pe.wait(m_ident)

    def split_weight(h, l, raw, loaded):
        act.wait(loaded)
        rounded = act.do(lambda e: e.activation(l, raw, ACT.Copy), "weight_round")
        dve.wait(rounded)
        low = dve.do(lambda e: e.tensor_tensor(l, raw, l.bitcast(F32), ALU.subtract), "weight_low")

        def finish():
            act.wait(low)
            return act.do(lambda e: e.activation(h, raw, ACT.Copy), "weight_high")
        return finish

    def transposes(bank, sources, name):
        pe.wait(bank.free)
        for i, src in enumerate(sources):
            r = lambda e, i=i, src=src: e.transpose(bank.ap[:, i * P:(i + 1) * P], src, ident[:, :])
            mark = pe.do(r, name if i == len(sources) - 1 else None)
        return mark

    def split_bank(bank, turned, high, low, free, name):
        act.wait(turned, free)
        m_high = act.do(lambda e: e.activation(high, bank.ap, ACT.Copy), name + "_high")
        dve.wait(m_high, turned, free)
        m_low = dve.do(lambda e: e.tensor_tensor(low, bank.ap, high.bitcast(F32), ALU.subtract), name + "_low")
        bank.free = [m_low]
        return [m_high, m_low]

    def products(bank, lhs, rhs, n, first=True, last=True):
        out_ap = bank
        return [lambda e, a=a, b=b, s=s, p=p: e.matmul(out_ap, a, b, start=s, stop=p)
                for a, b, s, p in ((lhs[0], rhs[0], first, False), (lhs[1], rhs[0], False, False),
                                   (lhs[0], rhs[1], False, last))]

    def layer_norm(src, pieces, dst, ready, k, name):
        st = stats[:, k, :]
        dve.wait(ready)
        for i, piece in enumerate(pieces):
            m = dve.do(lambda e, i=i, piece=piece: e.bn_stats(st[:, 6 * i:6 * i + 6], piece), name + "_stats")
        dve.wait(m)
        m = dve.do(lambda e: e.bn_aggr(st[:, 12:14], st[:, 0:6 * len(pieces)]), name + "_moments")
        pool.wait(m)
        m = pool.do(lambda e: e.tensor_scalar(st[:, 14:15], st[:, 13:14], 1.0, EPS, ALU.mult, ALU.add), name + "_var")
        pool.wait(m)
        m = pool.do(lambda e: e.tensor_tensor(st[:, 15:16], st[:, 14:15], half_power[:, 0:1], ALU.pow), name + "_rstd")
        dve.wait(m)
        return dve.do(lambda e: e.tensor_scalar(dst, src, st[:, 12:13], st[:, 15:16], ALU.subtract, ALU.mult),
                      name + "_normed")

    attend_plan = Plan(phase_base)
    wqkv_h, wqkv_raw = attend_plan.pair("wqkv_h", [P, KC, QKV])
    wqkv_l = attend_plan.tensor("wqkv_l", [P, KC, QKV], F32R)
    wo_h, wo_raw = attend_plan.pair("wo_h", [P, KC, DIM])
    wo_l = attend_plan.tensor("wo_l", [P, KC, DIM], F32R)
    attend_weights_end = attend_plan.at

    zone_start = {"wqkv": phase_base, "wo": phase_base + 2 * KC * QKV * 4, "late": attend_weights_end}
    zone_start["early"] = zone_start["late"] + LATE_BYTES
    zone_start["out"] = zone_start["early"] + EARLY_BYTES
    zone_start["top"] = zone_start["out"] + OUT_BYTES

    def new_zones():
        return {zone: [] for zone in zone_start}

    def compute_ends():
        return [q.last for q in (pe, act, dve, pool)]

    qk_banks = Slot(bank_pair)
    bank_slots = [Slot(b) for b in banks]

    weights_ready = {}

    def attend_weight_steps(l, wqkv_free, wo_free):
        raw, finishes = {}, {}
        wq = wqkv[l].rearrange("(c p) n -> p c n", p=P)
        cols = {part: slice(part * DIM, (part + 1) * DIM) for part in range(3)}
        parts = (2, 0, 1)

        def load_wqkv():
            sp.wait(wqkv_free)
            for part in parts:
                raw[part] = sp.do(lambda e, part=part: e.dma_start(wqkv_raw[:, :, cols[part]], wq[:, :, cols[part]]),
                                  f"wqkv_in{part}", 16)

        def load_wo():
            sp.wait(wo_free)
            raw["wo"] = sp.do(lambda e: e.dma_start(wo_raw[:, :, :], wo[l].rearrange("(c p) n -> p c n", p=P)), "wo_in", 16)

        def begin(part):
            h, lo, r = ((wo_h[:, :, :], wo_l[:, :, :], wo_raw[:, :, :]) if part == "wo" else
                        (wqkv_h[:, :, cols[part]], wqkv_l[:, :, cols[part]], wqkv_raw[:, :, cols[part]]))
            finishes[part] = split_weight(h, lo, r, raw[part])

        def finish(part):
            weights_ready[part] = finishes[part]()

        splits = []
        for part in parts:
            splits += [lambda part=part: begin(part), lambda part=part: finish(part)]
        return load_wqkv, splits, [load_wo, lambda: begin("wo"), lambda: finish("wo")]

    def band_phase(next_zones, next_start):
        plan = Plan(zone_start["late"])
        ctx_h = plan.tensor("ctx_h", [P, TPB, DIM], F32R)
        ctx_l = plan.tensor("ctx_l", [P, TPB, DIM], F32R)
        keyT_h = plan.tensor("keyT_h", [P, KC, SEQ], F32R)
        keyT_l = plan.tensor("keyT_l", [P, KC, SEQ], F32R)
        x_in = Ring([Slot(plan.tensor(f"x_in{i}", [P, DIM])) for i in range(7)])
        total = Ring([Slot(plan.tensor(f"ctx_total{i}", [P, DIM])) for i in range(2)])
        mixed = Slot(plan.tensor("mixed", [P, DIM]))
        ones = plan.tensor("ones", [P, P])
        soft = plan.tensor("soft", [P, 8, 8])
        assert plan.at <= zone_start["early"]
        plan = Plan(zone_start["early"])
        ctx_in = Ring([Slot(plan.tensor(f"ctx_in{i}", [P, DIM])) for i in range(3)])
        sum_in = Ring([Slot(plan.tensor(f"sum_in{i}", [P, DIM])) for i in range(2)])
        xn = Ring([Slot(plan.tensor(f"xn{i}", [P, DIM])) for i in range(2)])
        queryT = Ring([Slot(plan.tensor(f"queryT{i}", [P, 2, DIM], F32R)) for i in range(2)])
        assert plan.at >= zone_start["early"] + ATTEND_FIRST_BYTES
        ctx_sum = Slot(plan.tensor("ctx_sum", [P, DIM]))
        band01 = plan.tensor("band01", [P, WIN])
        key_mask = Slot(plan.tensor("key_mask", [P, SEQ], U8))
        key01 = Slot(plan.tensor("key01", [P, SEQ]))
        keep = Ring([Slot(plan.tensor(f"keep{i}", [P, WIN])) for i in range(2)])
        put = Ring([Slot(plan.tensor(f"put{i}", [P, WIN])) for i in range(2)])
        score = Slot(plan.tensor("score", [P, WIN]))
        prob = Ring([Slot(plan.tensor(f"prob{i}", [P, WIN])) for i in range(2)])
        probT = Ring([Slot(plan.tensor(f"probT{i}", [P, 2, WIN], F32R)) for i in range(2)])
        x1_out = Ring([Slot(plan.tensor(f"x1_out{i}", [P, DIM])) for i in range(2)])
        s_out = Ring([Slot(plan.tensor(f"s_out{i}", [P, DIM])) for i in range(2)])
        moments = plan.tensor("moments", [P, 8, 16])
        assert plan.at <= SBUF_END

        turn_banks = Ring([Slot(banks[0]), Slot(banks[1])])
        score_bank = Ring([Slot(banks[2]), Slot(banks[3])])
        probT_bank = Slot(banks[4])
        out_bank = Ring([Slot(banks[5]), Slot(bank_pair[:, 1, :])])
        total_bank = Slot(bank_pair[:, 0, :])

        m_ones = pool.do(lambda e: e.memset(ones[:, :], 1.0), "ones")
        m_band = sp.do(lambda e: e.dma_start(band01[:, :], consts["band01"]), "band01_in", 16)
        ctx_ready, read_by = [None] * TILES, [None] * TILES
        x_tile, x_normed, ctx_tile, sums, q_ready, masks, scored, totals, x1_tile, mixes, sum_tile = ({} for _ in range(11))
        probs, probTs = {}, {}
        key_state = {}

        def load(t):
            b, r = rows(t)
            slot = x_in.next()
            sp.wait(slot.free)
            x_tile[t] = (slot, sp.do(lambda e: e.dma_start(slot.ap[:, :], x[b, r:r + P, :]), f"x_in{t % 7}", 16))
            kslot = ctx_in.next()
            sp.wait(kslot.free)
            ctx_tile[t] = (kslot, sp.do(lambda e: e.dma_start(kslot.ap[:, :], ctx[b, r:r + P, :]), f"ctx_in{t % 3}", 16))

        def load_for_sum(t):
            b, r = rows(t)
            slot = sum_in.next()
            sp.wait(slot.free)
            sum_tile[t] = (slot, sp.do(lambda e: e.dma_start(slot.ap[:, :], ctx[b, r:r + P, :]), f"sum_in{t % 2}", 16))

        def add_to_sum(t):
            b, r = rows(t)
            slot, loaded = sum_tile.pop(t)
            pool.wait(loaded)
            if r == 0:
                pool.wait(ctx_sum.free)
                m = pool.do(lambda e: e.tensor_scalar(ctx_sum.ap[:, :], slot.ap[:, :], 1.0, 0.0, ALU.mult, ALU.add),
                            "ctx_sum")
            else:
                pool.wait(sums["last"])
                m = pool.do(lambda e: e.tensor_tensor(ctx_sum.ap[:, :], ctx_sum.ap[:, :], slot.ap[:, :], ALU.add),
                            "ctx_sum")
            sums["last"] = m
            slot.free = [m]

        def total_sum(t):
            if t % TPB < TPB - 1:
                return
            pe.wait(sums["last"], m_ones, total_bank.free)
            m = pe.do(lambda e: e.matmul(total_bank.ap, ones[:, :], ctx_sum.ap[:, :], start=True, stop=True), "total")
            ctx_sum.free = [m]
            tot = total.next()
            act.wait(m, tot.free)
            m = act.do(lambda e: e.activation(tot.ap[:, :], total_bank.ap, ACT.Copy), "total_out")
            total_bank.free = [m]
            totals[t // TPB] = (tot, m)

        def prepare_ctx(t):
            slot, loaded = ctx_tile[t]
            k = t % TPB
            pe.wait(loaded)
            bank = turn_banks.next()
            turned = transposes(bank, [slot.ap[:, c * P:(c + 1) * P] for c in range(KC)], "ctx_turned")
            old = [read_by[t - TPB + 1]] if t >= TPB else []
            view = Slot(bank.ap[:, :].rearrange("p (c n) -> p c n", c=KC))
            key_marks = split_bank(view, turned, keyT_h[:, :, k * P:(k + 1) * P], keyT_l[:, :, k * P:(k + 1) * P],
                                   old, "keyT")
            bank.free = view.free
            act.wait(loaded)
            m_h = act.do(lambda e: e.activation(ctx_h[:, k, :], slot.ap[:, :], ACT.Copy), "ctx_high")
            pool.wait(m_h)
            m_l = pool.do(lambda e: e.tensor_tensor(ctx_l[:, k, :], slot.ap[:, :], ctx_h[:, k, :].bitcast(F32),
                                                    ALU.subtract), "ctx_low")
            slot.free = [turned, m_h, m_l]
            ctx_ready[t] = key_marks + [m_h, m_l]

        def statistics(src, ready, st):
            dve.wait(ready)
            m = dve.do(lambda e: e.bn_stats(st[:, 0:6], src), "ln_stats")
            dve.wait(m)
            m = dve.do(lambda e: e.bn_aggr(st[:, 12:14], st[:, 0:6]), "ln_moments")
            pool.wait(m)
            m = pool.do(lambda e: e.tensor_scalar(st[:, 14:15], st[:, 13:14], 1.0, EPS, ALU.mult, ALU.add), "ln_var")
            pool.wait(m)
            m = pool.do(lambda e: e.tensor_tensor(st[:, 15:16], st[:, 14:15], half_power[:, 0:1], ALU.pow), "ln_rstd")
            pool.wait(m)
            return pool.do(lambda e: e.tensor_scalar(st[:, 14:15], st[:, 12:13], st[:, 15:16], -1.0, ALU.mult, ALU.mult),
                           "ln_offset")

        def normalise(src, dst, st, ready):
            act.wait(ready)
            return act.do(lambda e: e.activation(dst, src, ACT.Identity, bias=st[:, 14:15], scale=st[:, 15:16]),
                          "ln_normed_a")

        def query_statistics(t):
            slot, loaded = x_tile[t]
            x_normed[t] = statistics(slot.ap[:, :], loaded, moments[:, t % 4, :])

        def normalise_query(t):
            slot, _ = x_tile[t]
            n = xn.next()
            x_normed[t] = (n, normalise(slot.ap[:, :], n.ap[:, :], moments[:, t % 4, :], [x_normed[t], n.free]))

        def turn_query(t):
            n, m = x_normed.pop(t)
            pe.wait(m)
            bank = turn_banks.next()
            turned = transposes(bank, [n.ap[:, c * P:(c + 1) * P] for c in range(KC)], "x_turned")
            n.free = [turned]
            q = queryT.next()
            q_ready[t] = (q, split_bank(bank, turned, q.ap[:, 0, :], q.ap[:, 1, :], q.free, "queryT"))

        def window(t):
            k = t % TPB
            lo, hi = max(k - 1, 0), min(k + 1, TPB - 1)
            return lo, hi, (hi - lo + 1) * P, (lo - (k - 1)) * P

        def make_masks(t):
            lo, _, n, off = window(t)
            b, r = rows(t)
            if r == 0:
                sp.wait(key_mask.free)
                loaded = sp.do(lambda e: e.dma_start(key_mask.ap[:, :], mask[b].partition_broadcast(P)), "mask_in", 16)
                pool.wait(loaded, key01.free)
                key_state["ready"] = pool.do(lambda e: e.tensor_scalar(key01.ap[:, :], key_mask.ap[:, :], 1.0, 0.0,
                                                                       ALU.mult, ALU.add), "key01")
                key_mask.free = [key_state["ready"]]
            kp, pt = keep.next(), put.next()
            pool.wait(key_state["ready"], m_band, kp.free)
            m_keep = pool.do(lambda e: e.tensor_tensor(kp.ap[:, 0:n], band01[:, off:off + n],
                                                       key01.ap[:, lo * P:lo * P + n], ALU.mult), "keep")
            key01.free = [m_keep]
            pool.wait(m_keep, pt.free)
            m_put = pool.do(lambda e: e.tensor_scalar(pt.ap[:, 0:n], kp.ap[:, 0:n], -MASKED, MASKED,
                                                      ALU.mult, ALU.add), "put")
            masks[t] = (kp, pt, m_keep, m_put)

        def scores(t):
            k = t % TPB
            lo, hi, n, _ = window(t)
            q, ready = q_ready.pop(t)
            bank = score_bank.next()
            pe.wait(ready, [ctx_ready[t - k + i] for i in range(lo, hi + 1)], bank.free)
            keys = slice(lo * P, (hi + 1) * P)
            for c in range(KC):
                for f in products(bank.ap[:, 0:n], [q.ap[:, i, c * P:(c + 1) * P] for i in (0, 1)],
                                  (keyT_h[:, c, keys], keyT_l[:, c, keys]), n, c == 0, c == KC - 1):
                    m = pe.do(f, "scores")
            q.free = [m]
            scored[t] = (bank, m)

        def exponentials(t):
            n = window(t)[2]
            bank, m = scored.pop(t)
            kp, pt, m_keep, m_put = masks.pop(t)
            sm = soft[:, t % 8, :]
            dve.wait(m, m_keep, score.free)
            m = dve.do(lambda e: e.scalar_tensor_tensor(out=score.ap[:, 0:n], in0=bank.ap[:, 0:n], scalar=BAND_SCALE,
                                                        in1=kp.ap[:, 0:n], op0=ALU.mult, op1=ALU.mult), "kept")
            bank.free = kp.free = [m]
            dve.wait(m, m_put)
            m = dve.do(lambda e: e.tensor_tensor_reduce(score.ap[:, 0:n], score.ap[:, 0:n], pt.ap[:, 0:n], 1.0,
                                                        MASKED, ALU.add, ALU.max, sm[:, 0:1]), "score_max")
            pt.free = [m]
            dve.wait(m)
            m = dve.do(lambda e: e.tensor_scalar(sm[:, 1:2], sm[:, 0:1], -1.0, None, ALU.mult), "neg_max")
            p = prob.next()
            act.wait(m, p.free)
            m_out = act.do(lambda e: e.activation(sm[:, 2:3], masked_col[:, :], ACT.Exp, bias=sm[:, 1:2]), "masked_prob")
            m_exp = act.do(lambda e: e.activation(p.ap[:, 0:n], score.ap[:, 0:n], ACT.Exp, bias=sm[:, 1:2],
                                                  accum_out=sm[:, 3:4]), "prob")
            score.free = [m_exp]
            probs[t] = (p, [m_out, m_exp])

        def turn_probabilities(t):
            n = window(t)[2]
            p, ready = probs.pop(t)
            sm = soft[:, t % 8, :]
            dve.wait(ready)
            m_less = dve.do(lambda e: e.tensor_scalar(p.ap[:, 0:n], p.ap[:, 0:n], sm[:, 2:3], None, ALU.subtract),
                            "prob_less")
            m = dve.do(lambda e: e.scalar_tensor_tensor(out=sm[:, 4:5], in0=sm[:, 2:3], scalar=float(SEQ - n),
                                                        in1=sm[:, 3:4], op0=ALU.mult, op1=ALU.add), "band_den")
            dve.wait(m)
            m_r = dve.do(lambda e: e.reciprocal(sm[:, 5:6], sm[:, 4:5]), "band_rden")
            pe.wait(m_less)
            turned = transposes(probT_bank, [p.ap[:, i * P:(i + 1) * P] for i in range(n // P)], "probT")
            p.free = [turned]
            probTs[t] = (turned, m_r)

        def split_probabilities(t):
            n = window(t)[2]
            turned, m_r = probTs[t]
            view = Slot(probT_bank.ap[:, 0:n])
            pt = probT.next()
            ready = split_bank(view, turned, pt.ap[:, 0, 0:n], pt.ap[:, 1, 0:n], pt.free, "probT")
            probT_bank.free = view.free
            probTs[t] = (pt, ready, m_r)

        def mix(t):
            lo, _, n, _ = window(t)
            pt, ready, m_r = probTs.pop(t)
            bank = out_bank.next()
            pe.wait(ready, bank.free)
            for i in range(n // P):
                for f in products(bank.ap[:, :], [pt.ap[:, h, i * P:(i + 1) * P] for h in (0, 1)],
                                  (ctx_h[:, lo + i, :], ctx_l[:, lo + i, :]), DIM, i == 0, i == n // P - 1):
                    m = pe.do(f, "mix")
            pt.free = [m]
            read_by[t] = m
            mixes[t] = (bank, m, m_r)

        def add_x(t):
            bank, m, m_r = mixes.pop(t)
            sm = soft[:, t % 8, :]
            tot, m_tot = totals[t // TPB]
            dve.wait(m, m_tot, mixed.free)
            m = dve.do(lambda e: e.scalar_tensor_tensor(out=mixed.ap[:, :], in0=tot.ap[:, :], scalar=sm[:, 2:3],
                                                        in1=bank.ap[:, :], op0=ALU.mult, op1=ALU.add), "mixed")
            bank.free = [m]
            tot.free = [m]
            slot, _ = x_tile[t]
            x1 = x1_out.next()
            dve.wait(m, m_r, x1.free)
            m = dve.do(lambda e: e.scalar_tensor_tensor(out=x1.ap[:, :], in0=mixed.ap[:, :], scalar=sm[:, 5:6],
                                                        in1=slot.ap[:, :], op0=ALU.mult, op1=ALU.add), "x1")
            mixed.free = [m]
            slot.free = [m]
            b, r = rows(t)
            sp.wait(m)
            x1_stored[t] = sp.do(lambda e: e.dma_start(x1_dram[b, r:r + P, :], x1.ap[:, :]), f"x1_store{t % 2}", 16)
            x1_tile[t] = (x1, statistics(x1.ap[:, :], m, moments[:, 4 + t % 4, :]))

        def put_stream(t):
            x1, ready = x1_tile.pop(t)
            so = s_out.next()
            m = normalise(x1.ap[:, :], so.ap[:, :], moments[:, 4 + t % 4, :], [ready, so.free])
            b, r = rows(t)
            sp.wait(m)
            stream_stored[0][t] = sp.do(lambda e: e.dma_start(stream[0][b, 1 + r:1 + r + P, :], so.ap[:, :]),
                                        f"s_store{t % 2}", 16)
            x1.free = [x1_stored[t], m]
            so.free = [stream_stored[0][t]]

        load_wqkv, splits, wo_steps = attend_weight_steps(0, (), ())
        weight_steps = {WEIGHTS_AT: [load_wqkv, wo_steps[0]]}
        for i, step in enumerate(splits + wo_steps[1:]):
            weight_steps[WEIGHTS_AT + 3 + i] = [step]

        def weight_step(s):
            for step in weight_steps.get(s, ()):
                step()

        stages = [(mix, 5), (query_statistics, 1), (turn_probabilities, 4), (add_x, 5), (weight_step, 0),
                  (split_probabilities, 4), (turn_query, 2), (prepare_ctx, 1), (put_stream, 6), (make_masks, 2),
                  (scores, 3), (total_sum, 1 - SUM_AHEAD), (exponentials, 3), (normalise_query, 1)]
        load(0)
        for t in range(SUM_AHEAD):
            load_for_sum(t)
            if t:
                add_to_sum(t - 1)
        for s in range(TILES + 7):
            if s + 1 < TILES:
                load(s + 1)
            if s + SUM_AHEAD < TILES:
                load_for_sum(s + SUM_AHEAD)
            if s + SUM_AHEAD - 1 < TILES:
                add_to_sum(s + SUM_AHEAD - 1)
            if s == TILES + 3:
                next_zones["early"] += compute_ends()
                next_start()
            for stage, after in stages:
                if 0 <= s - after < TILES:
                    stage(s - after)
            if s == TILES + 5:
                next_zones["late"] += compute_ends()
        for zone in ("out", "top"):
            next_zones[zone] += compute_ends() + x1_stored[-2:] + stream_stored[0][-2:]
        for slot, used in zip(bank_slots, turn_banks.slots + score_bank.slots + [probT_bank, out_bank.slots[0]]):
            slot.free = used.free
        qk_banks.free = [total_bank.free, out_bank.slots[1].free]

    def attend_phase(l, src, dst, zones):
        sfx = f"_{l}"
        plan = Plan(zone_start["late"], zones["late"])
        kT = plan.tensor("kT" + sfx, [P, HEADS, SEQ], F32R)
        v_rows = plan.tensor("v_rows" + sfx, [P, TPB, HEADS * HD])
        qT = Ring([plan.slot(f"qT{i}" + sfx, [P, HEADS, 2, P], F32R) for i in range(2)])
        far = plan.tensor("far" + sfx, [P, WIN])
        score = Ring([plan.slot(f"lscore{i}" + sfx, [P, WIN]) for i in range(3)])
        prob = Ring([plan.slot(f"lprob{i}" + sfx, [P, WIN]) for i in range(3)])
        probT = Ring([plan.slot(f"lprobT{i}" + sfx, [P, WIN]) for i in range(3)])
        o_rows = plan.slot("o_rows" + sfx, [P, DIM])
        oT = plan.slot("oT" + sfx, [P, 2, DIM], F32R)
        assert plan.at <= zone_start["early"]
        plan = Plan(zone_start["early"], zones["early"])
        rope_cos = plan.tensor("rope_cos" + sfx, [P, TPB, 2 * HD])
        rope_sin = plan.tensor("rope_sin" + sfx, [P, TPB, 2 * HD])
        scales = plan.tensor("scales" + sfx, [P, 2 * HD])
        h_in = Ring([plan.slot(f"s_in{i}" + sfx, [P, DIM]) for i in range(2)])
        hT = Ring([plan.slot(f"hT{i}" + sfx, [P, 2, DIM], F32R) for i in range(2)])
        assert plan.at == zone_start["early"] + ATTEND_FIRST_BYTES <= zone_start["early"] + 2 * BLOCK_BYTES
        plan.free = zones["late"]
        square = plan.slot("square" + sfx, [P, 2, DIM])
        with_cos = plan.slot("with_cos" + sfx, [P, 2, DIM])
        with_sin = plan.slot("with_sin" + sfx, [P, 2, DIM])
        turned_qk = plan.slot("turned_qk" + sfx, [P, 2, DIM])
        assert plan.at <= zone_start["out"]
        plan = Plan(zone_start["out"], zones["out"])
        res_in = Ring([plan.slot(f"s_res{i}" + sfx, [P, DIM]) for i in range(2)])
        s_out = Ring([plan.slot(f"a_out{i}" + sfx, [P, DIM]) for i in range(2)])
        assert plan.at <= zone_start["top"]

        vy_bank = bank_slots[0]
        turn_banks = score_banks = Ring([bank_slots[i] for i in (2, 3, 4, 1)])
        o_bank = bank_slots[5]
        rope_ready, far_ready, m_zero = [], [], []

        def load_tables():
            sp.wait(zones["early"])
            sp.do(lambda e: e.dma_start(rope_cos[:, :, :], consts["rope_cos"]), "rope_in", 16)
            sp.do(lambda e: e.dma_start(rope_sin[:, :, :], consts["rope_sin"]), "rope_in", 16)
            sp.do(lambda e: e.dma_start(scales[:, 0:HD], q_scale[l].partition_broadcast(P)), "rope_in", 16)
            rope_ready.append(sp.do(lambda e: e.dma_start(scales[:, HD:], k_scale[l].partition_broadcast(P)),
                                    "rope_in", 16))

        def scale_tables():
            pool.wait(rope_ready)
            spread = scales[:, :].unsqueeze(1).to_broadcast([P, TPB, 2 * HD])
            for table in (rope_cos, rope_sin):
                rope_ready.append(pool.do(lambda e, table=table: e.tensor_tensor(table[:, :, :], table[:, :, :], spread,
                                                                                 ALU.mult), "rope_scaled"))

        def load_constants():
            sp.wait(zones["late"])
            far_ready.append(sp.do(lambda e: e.dma_start(far[:, :], consts["far"]), "far_in", 16))
            pool.wait(zones["late"], rope_ready)
            for s in qT.slots:
                pool.wait(m_zero)
                m_zero.append(pool.do(lambda e, s=s: e.memset(s.ap[HD:, :, 1, :].bitcast(F32), 0.0), "qT_zero"))
            pool.wait(m_zero)

        h_tile, res_tile, h_slot, v_ready, qk_ready, q_slot, k_ready = ({} for _ in range(7))
        attended, done = [None] * TILES, {}

        def load(t):
            b, r = rows(t)
            slot = h_in.next()
            sp.wait(slot.free, stream_stored[src][t], zero_rows[-1], stream_stored[src][t - 1] if t else None)
            sp.do(lambda e: e.dma_start(slot.ap[:, 0:HALF], stream[src][b, 1 + r:1 + r + P, 0:HALF]), f"s_in{t % 2}", 16)
            h_tile[t] = (slot, sp.do(lambda e: e.dma_start(slot.ap[:, HALF:], stream[src][b, r:r + P, HALF:]),
                                     f"s_in{t % 2}", 16))

        def load_res(t):
            b, r = rows(t)
            slot = res_in.next()
            sp.wait(slot.free)
            res_tile[t] = (slot, sp.do(lambda e: e.dma_start(slot.ap[:, :], stream[src][b, 1 + r:1 + r + P, :]),
                                       f"s_res{t % 2}", 16))

        def turn_h(t):
            slot, loaded = h_tile[t]
            pe.wait(loaded)
            bank = turn_banks.next()
            turned = transposes(bank, [slot.ap[:, c * P:(c + 1) * P] for c in range(KC)], "h_turned")
            slot.free = [turned]
            h = hT.next()
            ready = split_bank(bank, turned, h.ap[:, 0, :], h.ap[:, 1, :], h.free, "hT")
            h_slot[t] = (h, ready)

        def project_pieces(t):
            h, ready = h_slot[t]
            pieces = []
            for part, bank in ((2, vy_bank.ap[:, :]), (0, qk_banks.ap[:, 0, :]), (1, qk_banks.ap[:, 1, :])):
                for c in range(KC):
                    cols = slice(part * DIM, (part + 1) * DIM)
                    fs = products(bank, [h.ap[:, i, c * P:(c + 1) * P] for i in (0, 1)],
                                  (wqkv_h[:, c, cols], wqkv_l[:, c, cols]), DIM, c == 0, c == KC - 1)
                    pieces += [(part, c, i, f) for i, f in enumerate(fs)]
            marks = {}

            def emit(piece):
                part, c, i, f = piece
                if (c, i) == (0, 0):
                    pe.wait(ready, weights_ready[part], vy_bank.free if part == 2 else qk_banks.free)
                last = (c, i) == (KC - 1, 2)
                m = pe.do(f, "projected" if last else None)
                if last:
                    marks[part] = m
                    if part == 2:
                        old = attended[t - TPB + 2] if t >= TPB else None
                        act.wait(m, old, zones["late"])
                        v_ready[t] = act.do(lambda e: e.activation(v_rows[:, t % TPB, :], vy_bank.ap[:, :], ACT.Copy),
                                            "v_rows")
                        vy_bank.free = [v_ready[t]]
                    if part == 1:
                        h.free = [m]
                        qk_ready[t] = [marks[0], m]
            return [lambda p=p: emit(p) for p in pieces]

        def rope_steps(t):
            k = t % TPB
            nm = norm[:, t % 2, :]
            act.wait(qk_ready[t], square.free)
            flat = lambda s: s[:, :, :].rearrange("p a n -> p (a n)")
            m_sq = act.do(lambda e: e.activation(flat(square.ap), flat(qk_banks.ap), ACT.Square), "squared")
            table = lambda s: s[:, k, :].rearrange("p (a d) -> p a d", a=2).unsqueeze(2).to_broadcast([P, 2, HEADS, HD])
            by_head = lambda s: s[:, :, :].rearrange("p a (h d) -> p a h d", h=HEADS)
            heads16 = lambda s: s[:, :, :].rearrange("p a (h d) -> p (a h) d", d=HD)
            marks = {}

            def reduce():
                dve.wait(m_sq)
                m = dve.do(lambda e: e.tensor_reduce(nm[:, 0:16], heads16(square.ap), AX, ALU.add), "norm_sum")
                square.free = [m]
                pool.wait(m)
                m = pool.do(lambda e: e.tensor_scalar(nm[:, 0:16], nm[:, 0:16], NORM_FLOOR ** 2, 0.0, ALU.max, ALU.add),
                            "norm_floor")
                pool.wait(m)
                marks["r"] = pool.do(lambda e: e.tensor_tensor(nm[:, 16:32], nm[:, 0:16], half_power[:, :], ALU.pow),
                                     "norm_inverse")

            def cos():
                dve.wait(qk_ready[t], rope_ready, with_cos.free, m_sq)
                marks["cos"] = dve.do(lambda e: e.tensor_tensor(by_head(with_cos.ap), by_head(qk_banks.ap),
                                                                table(rope_cos), ALU.mult), "with_cos")

            def sin():
                dve.wait(with_sin.free)
                marks["sin"] = dve.do(lambda e: e.tensor_tensor(by_head(with_sin.ap), by_head(qk_banks.ap),
                                                                table(rope_sin), ALU.mult), "with_sin")
                qk_banks.free = [marks["sin"]]

            def combine():
                pool.wait(marks["cos"], marks["sin"], turned_qk.free)
                h2 = HD // 2
                for a, b in ((0, h2), (h2, 0)):
                    m = pool.do(lambda e, a=a, b=b: e.tensor_tensor(
                        heads16(turned_qk.ap)[:, :, a:a + h2], heads16(with_cos.ap)[:, :, a:a + h2],
                        heads16(with_sin.ap)[:, :, b:b + h2], ALU.add), "rotated")
                with_cos.free = with_sin.free = [m]
                pool.wait(m, marks["r"])
                inv = nm[:, 16:32].unsqueeze(2).to_broadcast([P, 16, HD])
                marks["qk"] = pool.do(lambda e: e.tensor_tensor(heads16(turned_qk.ap), heads16(turned_qk.ap), inv,
                                                                ALU.mult), "qk_scaled")
            return [reduce, cos, sin, combine], marks

        lo, hi = slice(0, HD), slice(HD, P)

        def pairs(bank, half):
            return bank.ap[half, :].rearrange("p (i n) -> p i n", i=4)

        def turn_q(t, scaled):
            pe.wait(scaled)
            bank, q = turn_banks.next(), qT.next()
            turned = transposes(bank, [turned_qk.ap[:, 0, i * P:(i + 1) * P] for i in range(4)], "q_turned")
            marks = []
            act.wait(turned, q.free)
            dve.wait(turned, q.free)
            for odd, here in ((0, lo), (1, hi)):
                source = pairs(bank, here)
                for where in (here, hi if here is lo else lo):
                    marks.append(act.do(lambda e, source=source, where=where, odd=odd: e.activation(
                        q.ap[where, odd::2, 0, :], source, ACT.Copy), "qT_high"))
                dve.wait(marks[-1])
                marks.append(dve.do(lambda e, source=source, here=here, odd=odd: e.tensor_tensor(
                    q.ap[lo, odd::2, 1, :], source, q.ap[here, odd::2, 0, :].bitcast(F32), ALU.subtract), "qT_low"))
            bank.free = [marks[-1]]
            q_slot[t] = (q, marks + m_zero)

        def turn_k(t):
            k = t % TPB
            bank = turn_banks.next()
            turned = transposes(bank, [turned_qk.ap[:, 1, i * P:(i + 1) * P] for i in range(4)], "k_turned")
            turned_qk.free = [turned]
            old = attended[t - TPB + 2] if t >= TPB else None
            act.wait(turned, old, zones["late"])
            dve.wait(turned, old, zones["late"])
            cols = slice(k * P, (k + 1) * P)
            marks = []
            for odd, here in ((0, lo), (1, hi)):
                source = pairs(bank, here)
                m = act.do(lambda e, source=source, odd=odd: e.activation(kT[lo, odd::2, cols], source, ACT.Copy),
                           "kT_high")
                dve.wait(m)
                marks += [m, dve.do(lambda e, source=source, odd=odd: e.tensor_tensor(
                    kT[hi, odd::2, cols], source, kT[lo, odd::2, cols].bitcast(F32), ALU.subtract), "kT_low")]
            bank.free = [marks[-1]]
            k_ready[t] = marks

        def normalise_out(t):
            m_den, m_mix = done[t]
            sm = small[:, t % 2, :]
            dve.wait(m_den)
            m = dve.do(lambda e: e.reciprocal(sm[:, 16:24], sm[:, 8:16]), "lrden")
            dve.wait(m, m_mix, o_rows.free)
            m = dve.do(lambda e: e.tensor_tensor(
                o_rows.ap[:, :].rearrange("p (h d) -> p h d", h=HEADS),
                o_bank.ap[:, :].rearrange("p (h d) -> p h d", h=HEADS),
                sm[:, 16:24].unsqueeze(2).to_broadcast([P, HEADS, HD]), ALU.mult), "o_rows")
            o_bank.free = [m]
            done[t] = m

        def turn_out(t):
            pe.wait(done[t])
            bank = turn_banks.next()
            turned = transposes(bank, [o_rows.ap[:, c * P:(c + 1) * P] for c in range(KC)], "o_turned")
            o_rows.free = [turned]
            done[t] = split_bank(bank, turned, oT.ap[:, 0, :], oT.ap[:, 1, :], oT.free, "oT")

        def project_out(t, half):
            if half == 0:
                pe.wait(done[t], weights_ready["wo"], vy_bank.free)
            for c in (0, 1) if half == 0 else (2, 3):
                for f in products(vy_bank.ap[:, :], [oT.ap[:, i, c * P:(c + 1) * P] for i in (0, 1)],
                                  (wo_h[:, c, :], wo_l[:, c, :]), DIM, c == 0, c == KC - 1):
                    m = pe.do(f, "wo_done")
            if half == 1:
                oT.free = [m]
                done[t] = m

        def add_residual(t):
            slot, loaded = res_tile[t]
            so = s_out.next()
            dve.wait(done[t], loaded, so.free)
            m = dve.do(lambda e: e.tensor_tensor(so.ap[:, :], vy_bank.ap[:, :], slot.ap[:, :], ALU.add), "a_out")
            vy_bank.free = [m]
            slot.free = [m]
            b, r = rows(t)
            sp.wait(m)
            stream_stored[dst][t] = sp.do(lambda e: e.dma_start(stream[dst][b, 1 + r:1 + r + P, :], so.ap[:, :]),
                                          f"a_store{t % 2}", 16)
            so.free = [stream_stored[dst][t]]

        rope_slots = (0, 1, 2, 4)
        projected_by = (6, 7, 11, 14, 18, 22, 25, 29, 32, 36)
        act_copies = (1, 2, 3, 5, 6, 8)
        at_slot = dict(normalise_out=0, turn_out=2, turn_h=3, project_out=(5, 6),
                       add_residual=7, turn_q=6, turn_k=8)

        def step(s, tail_work):
            t, tail = s - 2, s - 3
            live = 0 <= t < TILES
            ended = 0 <= tail < TILES
            pieces = project_pieces(s) if s < TILES else []
            fillers, marks = rope_steps(s - 1) if 1 <= s <= TILES else ([], None)
            if live:
                k = t % TPB
                w = min(k, 2) + 1
                n = w * P
                first = (k - w + 1) * P
                q, q_marks = q_slot[t]
                sm = small[:, t % 2, :]
                keys_ready = [k_ready[t - i] for i in range(w)]
                load_res(t)
            if s + 2 < TILES:
                load(s + 2)
            soft = {}
            for i in range(HEADS + 2):
                if ended and i == at_slot["normalise_out"]:
                    normalise_out(tail)
                if live and i < HEADS:
                    bank, sc, p = score_banks.next(), score.next(), prob.next()
                    pe.wait(q_marks, keys_ready, bank.free)
                    for part in (0, 1):
                        m = pe.do(lambda e, part=part, i=i, bank=bank: e.matmul(
                            bank.ap[:, 0:n], q.ap[:, i, part, :], kT[:, i, first:first + n],
                            start=(part == 0), stop=(part == 1)), "lscores" if part else None)
                    if i == HEADS - 1:
                        q.free = [m]
                    dve.wait(m, sc.free, far_ready)
                    m = dve.do(lambda e, i=i, bank=bank, sc=sc: e.tensor_tensor_reduce(
                        sc.ap[:, 0:n], bank.ap[:, 0:n], far[:, WIN - n:], 1.0, BIG, ALU.add, ALU.min,
                        sm[:, i:i + 1]), "lmax")
                    bank.free = [m]
                    act.wait(m, p.free)
                    m = act.do(lambda e, i=i, sc=sc, p=p: e.activation(
                        p.ap[:, 0:n], sc.ap[:, 0:n], ACT.Exp, bias=sm[:, i:i + 1], scale=-1.0,
                        accum_out=sm[:, 8 + i:9 + i]), "lprob")
                    sc.free = [m]
                    soft[i] = (p, m)
                    m_den = m
                if marks and i == at_slot["turn_q"]:
                    turn_q(s - 1, marks["qk"])
                if marks and i == at_slot["turn_k"]:
                    turn_k(s - 1)
                if fillers and i in rope_slots:
                    fillers[rope_slots.index(i)]()
                for f in pieces[projected_by[i - 1] if i else 0:projected_by[i]]:
                    f()
                if ended and i == at_slot["turn_out"]:
                    turn_out(tail)
                if live and 1 <= i <= HEADS:
                    p, m = soft[i - 1]
                    pe.wait(m)
                    bank, pt = turn_banks.next(), probT.next()
                    turned = transposes(bank, [p.ap[:, j * P:(j + 1) * P] for j in range(w)], "lprobT")
                    p.free = [turned]
                    eng = act if i in act_copies else dve
                    eng.wait(turned, pt.free)
                    if eng is act:
                        m = act.do(lambda e, bank=bank, pt=pt: e.activation(pt.ap[:, 0:n], bank.ap[:, 0:n], ACT.Copy),
                                   "lprobT_a")
                    else:
                        m = dve.do(lambda e, bank=bank, pt=pt: e.tensor_copy(pt.ap[:, 0:n], bank.ap[:, 0:n]),
                                   "lprobT_v")
                    bank.free = [m]
                    soft[i - 1] = (pt, m)
                if live and i >= 2:
                    h = i - 2
                    pt, m = soft[h]
                    pe.wait(m, [v_ready[t - j] for j in range(w)], o_bank.free)
                    for j in range(w):
                        m = pe.do(lambda e, j=j, h=h, pt=pt: e.matmul(
                            o_bank.ap[:, h * HD:(h + 1) * HD], pt.ap[:, j * P:(j + 1) * P],
                            v_rows[:, k - w + 1 + j, h * HD:(h + 1) * HD], start=(h == 0 and j == 0),
                            stop=(j == w - 1), skip_group_check=True), "lmix" if j == w - 1 else None)
                    pt.free = [m]
                if i == at_slot["turn_h"] and s + 1 < TILES:
                    turn_h(s + 1)
                if ended and i in at_slot["project_out"]:
                    project_out(tail, at_slot["project_out"].index(i))
                if ended and i == at_slot["add_residual"]:
                    add_residual(tail)
                for work in tail_work.get((s, i), ()):
                    work()
            if live:
                attended[t] = m
                done[t] = (m_den, m)

        def start():
            load(0)
            load_tables()
            load(1)

        def run(next_zones, tail_work):
            turn_h(0)
            scale_tables()
            load_constants()
            for s in range(TILES + 3):
                step(s, tail_work)
                if s == TILES - 1:
                    next_zones["wqkv"] += qk_ready[s]
                if s == TILES:
                    next_zones["early"] += turned_qk.free
            ends = compute_ends()
            for zone in ("wo", "late", "out"):
                next_zones[zone] += ends
            next_zones["out"] += stream_stored[dst][-2:]
        return start, run

    def ffn_phase(l, src, dst, zones):
        sfx = f"_f{l}"
        block_h, block_raw, block_l, block_zone = ([None] * HC for _ in range(4))

        def place_block(plan, j):
            size = 2 * KC * hid_rows(j) + DIM
            block_h[j], block_raw[j] = plan.pair(f"w_h{j}" + sfx, [P, size])
            block_l[j] = plan.tensor(f"w_l{j}" + sfx, [P, size], F32R)
            block_zone[j] = plan.free

        full = HC - 1
        plan = Plan(zone_start["wqkv"], zones["wqkv"])
        hT_even = plan.slot("fhT0" + sfx, [P, 2, KC, GROUP * P], F32R)
        place_block(plan, 1)
        place_block(plan, 2)
        h_in = Ring([plan.slot(f"h_in{i}" + sfx, [P, DIM]) for i in range(2)])
        h_norm = Ring([plan.slot(f"h_norm{i}" + sfx, [P, DIM]) for i in range(2)])
        assert plan.at <= zone_start["wo"]
        plan = Plan(zone_start["wo"], zones["wo"])
        place_block(plan, 5)
        gate = Ring([plan.slot(f"gate{i}" + sfx, [P, GROUP * P]) for i in range(2)])
        assert plan.at <= zone_start["late"]
        plan = Plan(zone_start["late"], zones["late"])
        for j in range(6, HC):
            place_block(plan, j)
        hT = Ring([hT_even, plan.slot("fhT1" + sfx, [P, 2, KC, GROUP * P], F32R)])
        bias2 = plan.tensor("bias2" + sfx, [P, DIM])
        uT_late = [plan.slot(f"uT{i}" + sfx, [P, 2, GROUP * P], F32R) for i in range(2)]
        assert plan.at <= zone_start["early"]
        plan = Plan(zone_start["early"], zones["early"])
        place_block(plan, 3)
        place_block(plan, 4)
        gain = plan.tensor("gain" + sfx, [P, DIM])
        shift = plan.tensor("shift" + sfx, [P, DIM])
        u = Ring([plan.slot(f"u{i}" + sfx, [P, GROUP * P]) for i in range(2)])
        uT = Ring(uT_late + [plan.slot("uT2" + sfx, [P, 2, GROUP * P], F32R)])
        assert plan.at <= zone_start["out"]
        add_x1 = l == DEPTH - 1
        plan = Plan(zone_start["out"], zones["out"])
        res = Ring([plan.slot(f"res{i}" + sfx, [P, DIM]) for i in range(3)])
        x1_in = Ring([plan.slot(f"x1_in{i}" + sfx, [P, DIM]) for i in range(1)]) if add_x1 else None
        assert plan.at <= zone_start["top"]
        plan = Plan(zone_start["top"], zones["top"])
        place_block(plan, 0)
        bias1 = plan.tensor("bias1" + sfx, [P, 2, HC])
        assert plan.at <= SBUF_END

        y_banks = [bank_slots[0], Slot(bank_pair[:, 0, :]), Slot(bank_pair[:, 1, :]), bank_slots[1]]
        h_banks = Ring([bank_slots[2], bank_slots[3], bank_slots[4]])

        def w1_part(blocks, j, half, c):
            n = hid_rows(j)
            at = (half * KC + c) * n
            return blocks[j][:, at:at + n]

        def w2_part(blocks, j):
            n = hid_rows(j)
            return blocks[j][0:n, 2 * KC * n:2 * KC * n + DIM]

        vectors = {}

        def load_bias1():
            sp.wait(zones["top"])
            for half in (0, 1):
                v = b1[l, half * HID:(half + 1) * HID]
                sp.do(lambda e, v=v, half=half: e.dma_start(bias1[:, half, 0:full],
                                                            v[0:full * P].rearrange("(j p) -> p j", p=P)), "bias1_in", 16)
                vectors["bias1"] = sp.do(lambda e, v=v, half=half: e.dma_start(
                    bias1[0:hid_rows(full), half, full:HC], v[full * P:HID].unsqueeze(1)), "bias1_in", 16)

        def load_gain():
            sp.wait(zones["early"])
            sp.do(lambda e: e.dma_start(gain[:, :], ln_g[l].partition_broadcast(P)), "gain_in", 16)
            vectors["gain"] = sp.do(lambda e: e.dma_start(shift[:, :], ln_b[l].partition_broadcast(P)), "gain_in", 16)

        def load_bias2():
            sp.wait(zones["late"])
            vectors["bias2"] = sp.do(lambda e: e.dma_start(bias2[:, :], b2[l].partition_broadcast(P)), "bias2_in", 16)

        w1v = w1[l].rearrange("(c p) n -> p c n", p=P)
        block_loaded, block_ready, block_finish = {}, {}, {}

        def load_block(j):
            n = hid_rows(j)
            sp.wait(block_zone[j])
            for half in (0, 1):
                to = block_raw[j][:, half * KC * n:(half + 1) * KC * n].rearrange("p (c n) -> p c n", n=n)
                start = half * HID + j * P
                sp.do(lambda e, to=to, start=start: e.dma_start(to, w1v[:, :, start:start + n]), f"w_in{j}", 16)
            block_loaded[j] = sp.do(lambda e: e.dma_start(w2_part(block_raw, j), w2[l, j * P:j * P + n, :]), f"w_in{j}", 16)

        def split_begin(j):
            n = hid_rows(j)
            if n == P:
                pieces = [[b[j][:, :] for b in (block_h, block_l, block_raw)]]
            else:
                pieces = [[b[j][:, 0:2 * KC * n] for b in (block_h, block_l, block_raw)],
                          [w2_part(b, j) for b in (block_h, block_l, block_raw)]]
            block_finish[j] = [split_weight(h, low, raw, block_loaded[j]) for h, low, raw in pieces]

        def split_finish(j):
            block_ready[j] = [finish() for finish in block_finish[j]]

        h_slots, h_marks = {}, {}

        tiles = {}

        def load(t):
            b, r = rows(t)
            slot = h_in.next()
            sp.wait(slot.free, stream_stored[src][t], zero_rows[-1], stream_stored[src][t - 1] if t else None)
            sp.do(lambda e: e.dma_start(slot.ap[:, 0:HALF], stream[src][b, 1 + r:1 + r + P, 0:HALF]), f"h_in{t % 2}", 16)
            loaded = sp.do(lambda e: e.dma_start(slot.ap[:, HALF:], stream[src][b, r:r + P, HALF:]), f"h_in{t % 2}", 16)
            tiles[t] = (slot, loaded)

        def normalise(t):
            slot, loaded = tiles[t]
            hn = h_norm.next()
            dve.wait(hn.free)
            m = layer_norm(slot.ap[:, :], [slot.ap[:, :]], hn.ap[:, :], loaded, t % 2, "ln")
            slot.free = [m]
            pool.wait(m, vectors["gain"])
            m = pool.do(lambda e: e.tensor_tensor(hn.ap[:, :], hn.ap[:, :], gain[:, :], ALU.mult), "gained")
            pool.wait(m)
            m = pool.do(lambda e: e.tensor_tensor(hn.ap[:, :], hn.ap[:, :], shift[:, :], ALU.add), "shifted")
            tiles[t] = (hn, m)

        def turn(t, turn_bank=bank_slots[5]):
            g, i = divmod(t, GROUP)
            hn, m = tiles.pop(t)
            pe.wait(m)
            turned = transposes(turn_bank, [hn.ap[:, c * P:(c + 1) * P] for c in range(KC)], "fh_turned")
            hn.free = [turned]
            if i == 0:
                h_slots[g], h_marks[g] = hT.next(), []
            h = h_slots[g]
            view = Slot(turn_bank.ap[:, :].rearrange("p (c n) -> p c n", c=KC))
            h_marks[g] += split_bank(view, turned, h.ap[:, 0, :, i * P:(i + 1) * P], h.ap[:, 1, :, i * P:(i + 1) * P],
                                     h.free, "fhT")
            turn_bank.free = view.free

        def up(g, j):
            n = hid_rows(j)
            h = h_slots[g]
            marks, bank_of = {}, {}
            for half in (1, 0):
                bank = h_banks.next()
                bank_of[half] = bank
                pe.wait(h_marks[g], block_ready[j], bank.free)
                for c in range(KC):
                    fs = [lambda e, a=a, b=b, s=s, p=p, bank=bank: e.matmul(bank.ap[0:n, :], a, b, start=s, stop=p)
                          for a, b, s, p in (
                              (w1_part(block_h, j, half, c), h.ap[:, 0, c, :], c == 0, False),
                              (w1_part(block_h, j, half, c), h.ap[:, 1, c, :], False, False),
                              (w1_part(block_l, j, half, c), h.ap[:, 0, c, :], False, c == KC - 1))]
                    for f in fs:
                        m = pe.do(f, "up")
                marks[half] = m
            if j == HC - 1:
                h.free = [m]
            gt, uu, ut = gate.next(), u.next(), uT.next()
            act.wait(marks[1], gt.free, vectors["bias1"])
            m = act.do(lambda e: e.activation(gt.ap[0:n, :], bank_of[1].ap[0:n, :], ACT.Gelu,
                                              bias=bias1[0:n, 1, j:j + 1]), "gate")
            bank_of[1].free = [m]
            dve.wait(m, marks[0], uu.free, vectors["bias1"])
            m = dve.do(lambda e: e.scalar_tensor_tensor(out=uu.ap[0:n, :], in0=bank_of[0].ap[0:n, :],
                                                        scalar=bias1[0:n, 0, j:j + 1], in1=gt.ap[0:n, :],
                                                        op0=ALU.add, op1=ALU.mult), "u")
            bank_of[0].free = gt.free = [m]
            act.wait(m, ut.free)
            m_h = act.do(lambda e: e.activation(ut.ap[0:n, 0, :], uu.ap[0:n, :], ACT.Copy), "uT_high")
            dve.wait(m_h, ut.free)
            m_l = dve.do(lambda e: e.tensor_tensor(ut.ap[0:n, 1, :], uu.ap[0:n, :], ut.ap[0:n, 0, :].bitcast(F32),
                                                   ALU.subtract), "uT_low")
            uu.free = [m_l]
            return ut, [m_h, m_l]

        def down(j, ut, ready):
            n = hid_rows(j)
            pe.wait(ready, block_ready[j])
            marks = []
            for i in range(GROUP):
                if j == 0:
                    pe.wait(y_banks[i].free)
                for f in products(y_banks[i].ap, [ut.ap[0:n, h, i * P:(i + 1) * P] for h in (0, 1)],
                                  (w2_part(block_h, j), w2_part(block_l, j)), DIM, j == 0, j == HC - 1):
                    m = pe.do(f, "down")
                marks.append(m)
            ut.free = [m]
            return marks

        residual = {}

        def load_residual(t):
            b, r = rows(t)
            slot = res.next()
            sp.wait(slot.free)
            loaded = sp.do(lambda e: e.dma_start(slot.ap[:, :], stream[src][b, 1 + r:1 + r + P, :]), f"res_in{t % 3}", 16)
            pool.wait(loaded, vectors["bias2"])
            m = pool.do(lambda e: e.tensor_tensor(slot.ap[:, :], slot.ap[:, :], bias2[:, :], ALU.add), "res_bias")
            if add_x1:
                xs = x1_in.next()
                sp.wait(xs.free, x1_stored[t])
                loaded = sp.do(lambda e: e.dma_start(xs.ap[:, :], x1_dram[b, r:r + P, :]), "x1_in", 16)
                pool.wait(loaded, m)
                m = pool.do(lambda e: e.tensor_tensor(slot.ap[:, :], slot.ap[:, :], xs.ap[:, :], ALU.add), "res_x1")
                xs.free = [m]
            residual[t] = (slot, m)

        def finish(t, m_y):
            b, r = rows(t)
            i = t % GROUP
            slot, m = residual.pop(t)
            dve.wait(m, m_y)
            m = dve.do(lambda e: e.tensor_tensor(slot.ap[:, :], y_banks[i].ap, slot.ap[:, :], ALU.add), "f_out")
            y_banks[i].free = [m]
            sp.wait(m)
            target = out[b, r:r + P, :] if add_x1 else stream[dst][b, 1 + r:1 + r + P, :]
            m = sp.do(lambda e: e.dma_start(target, slot.ap[:, :]), f"f_store{t % 3}", 16)
            slot.free = [m]
            if not add_x1:
                stream_stored[dst][t] = m

        def finish_group(g, marks):
            for i in range(GROUP):
                if i == GROUP - 1:
                    load_residual(g * GROUP + i)
                finish(g * GROUP + i, marks[i])

        def run(next_zones, tail_work):
            y_banks[1].free = y_banks[2].free = qk_banks.free
            load_bias2()
            for j in range(5, HC):
                load_block(j)
            pending = None
            for g in range(GROUPS):
                for j in range(HC):
                    if g == 0 and 3 <= j + 1 < HC:
                        split_finish(j + 1)
                    ut, ready = up(g, j)
                    if g == 0:
                        if 3 <= j + 2 < HC:
                            split_begin(j + 2)
                    if pending:
                        marks = down(*pending)
                        if j == 0:
                            finish_group(g - 1, marks)
                    pending = (j, ut, ready)
                    i, later = divmod(j, 2)
                    following = (g + 1) * GROUP + i
                    if g + 1 < GROUPS:
                        if later == 0 and i < GROUP:
                            load(following)
                        if later == 1 and i < GROUP:
                            normalise(following)
                        if later == 1 and 1 <= i <= GROUP:
                            turn(following - 1)
                    if later == 0 and 2 <= i < 5:
                        load_residual(g * GROUP + i - 2)
                    if g == GROUPS - 1:
                        if j == 3:
                            next_zones["wqkv"] += marks
                        if j == 5:
                            next_zones["early"] += marks
                        for work in tail_work.get(j, ()):
                            work()
            finish_group(GROUPS - 1, down(*pending))
            qk_banks.free = [y_banks[1].free, y_banks[2].free]
            ends = compute_ends()
            for zone in ("wo", "late", "out", "top"):
                next_zones[zone] += ends
            if not add_x1:
                next_zones["out"] += stream_stored[dst][-3:]

        side = bank_slots[1]
        before = {
            (TILES - 1, 0): [lambda: load_block(0), load_bias1],
            (TILES - 1, 5): [lambda: split_begin(0)],
            (TILES - 1, 7): [lambda: split_finish(0)],
            (TILES, 0): [lambda: load(0), lambda: load(1), lambda: load_block(1), lambda: load_block(2)],
            (TILES, 2): [lambda: split_begin(1)],
            (TILES, 4): [lambda: split_finish(1)],
            (TILES, 5): [lambda: split_begin(2)],
            (TILES, 7): [lambda: split_finish(2)],
            (TILES + 1, 0): [load_gain, lambda: load_block(3), lambda: load_block(4), lambda: normalise(0), lambda: load(2)],
            (TILES + 1, 2): [lambda: normalise(1), lambda: load(3)],
            (TILES + 1, 3): [lambda: turn(0, side)],
            (TILES + 1, 4): [lambda: normalise(2), lambda: turn(1, side)],
            (TILES + 1, 6): [lambda: normalise(3), lambda: turn(2, side)],
            (TILES + 1, 7): [lambda: turn(3, side)],
        }
        return before, run

    def everything():
        return [(s, s.value) for s in signals.values()]

    attend_zones, ffn_zones = ([new_zones() for _ in range(DEPTH + 1)] for _ in range(2))
    for attend_z, ffn_z in zip(attend_zones, ffn_zones):
        ffn_z["top"] = attend_z["top"]
    start, run = attend_phase(0, 0, 1, attend_zones[0])
    band_phase(attend_zones[0], start)
    work = {}
    for l in range(DEPTH):
        before_ffn, run_ffn = ffn_phase(l, 2 * l + 1, 2 * l + 2, ffn_zones[l])
        run(ffn_zones[l], {**work, **before_ffn})
        if l + 1 < DEPTH:
            z = attend_zones[l + 1]
            start, run = attend_phase(l + 1, 2 * l + 2, 2 * l + 3, z)
            load_wqkv, splits, wo_steps = attend_weight_steps(l + 1, z["wqkv"], z["wo"])
            run_ffn(z, {3: [load_wqkv], 5: [start, splits[0]], 6: [splits[1]], 7: [splits[2]], 8: [splits[3]],
                        9: [splits[4]], 10: [splits[5]]})
            wo_steps[0]()
            work = {(0, 5): [wo_steps[1]], (0, 9): [wo_steps[2]]}
        else:
            run_ffn(attend_zones[l + 1], {})
    sp.wait(everything())

    with nc.allow_non_contiguous_dma(reason="bias columns"), nc.Block() as block:
        block.sync(sp.run)
        block.tensor(pe.run)
        block.scalar(act.run)
        block.vector(dve.run)
        block.gpsimd(pool.run)


def shape_constants():
    f = np.float32
    i, j = np.arange(P)[:, None], np.arange(WIN)[None, :]
    band01 = (np.abs(i - (j - P)) <= P).astype(f)
    back = i - (j - 2 * P)
    far = np.where((back < 0) | (back > 2 * P), f(BIG), f(0)).astype(f)
    half_idx = np.arange(0, HD, 2, dtype=f)
    inv_freq = f(1.0) / f(10000.0) ** (half_idx / f(HD))
    t = np.arange(SEQ, dtype=f)
    freqs = t[:, None] * inv_freq[None, :]
    base = (half_idx + f(0.4 * HD)) / f(1.4 * HD)
    power = (t - f(SEQ // 2)) / f(128.0)
    scale = base[None, :] ** power[:, None]
    cos, sin = np.cos(freqs), np.sin(freqs)
    c, s = [], []
    for sc, m in ((scale, -QK_SCALE), (f(1.0) / scale, 1.0)):
        c += [cos * sc * f(m), cos * sc * f(m)]
        s += [sin * sc * f(m), -sin * sc * f(m)]
    tile = lambda parts: np.ascontiguousarray(
        np.concatenate(parts, 1).astype(f).reshape(TPB, P, 2 * HD).transpose(1, 0, 2))
    return {"ident": np.eye(P, dtype=f), "zeros": np.zeros((BATCH, DIM), f), "band01": band01, "far": far,
            "rope_cos": tile(c), "rope_sin": tile(s)}


_INS = ["x", "ctx_1024", "mask_BxS2_bf1", "L0_ffn_wqkv", "L0_ffn_q_scale", "L0_ffn_k_scale", "L0_ffn_wo",
        "L0_ffn_ln_g", "L0_ffn_ln_b", "L0_ffn_w1", "L0_ffn_b1", "L0_ffn_w2", "L0_ffn_b2"]


def kernel(**inputs):
    import concourse.bacc as bacc
    from concourse.bass_utils import run_bass_kernel_spmd

    nc = bacc.Bacc("TRN2", target_bir_lowering=False, num_devices=1)
    arrays = {}

    def declare(name, a):
        a = np.ascontiguousarray(a)
        if a.dtype.kind == "b":
            a = a.view(np.uint8)
        arrays[name] = a
        return nc.dram_tensor(name, a.shape, mybir.dt.from_np(a.dtype), kind="ExternalInput").ap()

    args = [declare(f"in_{name}", inputs[name]) for name in _INS]
    consts = {name: declare(f"const_{name}", a) for name, a in shape_constants().items()}
    out = nc.dram_tensor("out_0", (BATCH, SEQ, DIM), F32, kind="ExternalOutput").ap()
    build(nc, *args, consts, out)
    r = run_bass_kernel_spmd(nc, [arrays], core_ids=[0])
    return r.results[0]["out_0"]
```
